# Optimizing a Trainium2 kernel written in Bass

```python
import numpy as np
import jax
import jax.numpy as jnp

def _softmax(x, axis=-1):
    return jax.nn.softmax(x, axis=axis)

def _gelu(x):
    return jax.nn.gelu(x, approximate=True)

def _silu(x):
    return jax.nn.silu(x)

def _sigmoid(x):
    return jax.nn.sigmoid(x)

def _layernorm(x, axis=-1, eps=1e-05):
    m = jnp.mean(x, axis=axis, keepdims=True)
    v = jnp.var(x, axis=axis, keepdims=True)
    return (x - m) / jnp.sqrt(v + eps)

def _scatter_add(tgt, idx, src, axis=0):
    return tgt.at[idx].add(src)

def _segment_sum(src, seg, n):
    return jax.ops.segment_sum(src, seg, n)
kernel_name = 'mk_prb_d2_jaxref_r8_69645a'

def setup_inputs(seed: int=0):
    np.random.seed(seed)
    _w = jnp.asarray

    def _L0_attn_setup():
        import jax, jax.numpy as jnp
        import numpy as np
        EMBED = 512
        NUM_Q_HEADS = 32
        NUM_KV_HEADS = 8
        HEAD_DIM = EMBED // NUM_Q_HEADS
        N_REP = 4
        key = jax.random.key(seed)
        k_x, k_q, k_k, k_v, k_o = jax.random.split(key, 5)
        B, T = (2, 256)
        kv_dim = HEAD_DIM * NUM_KV_HEADS
        s = 1.0 / np.sqrt(EMBED)
        return {'x': jax.random.normal(k_x, (B, T, EMBED), dtype=jnp.float32), 'Wq': jax.random.normal(k_q, (EMBED, EMBED), dtype=jnp.float32) * s, 'Wk': jax.random.normal(k_k, (kv_dim, EMBED), dtype=jnp.float32) * s, 'Wv': jax.random.normal(k_v, (kv_dim, EMBED), dtype=jnp.float32) * s, 'Wo': jax.random.normal(k_o, (EMBED, EMBED), dtype=jnp.float32) * s}
    _L0_attn_in = _L0_attn_setup()

    def _L0_ffn_setup():
        import jax, jax.numpy as jnp
        import numpy as np
        HIDDEN_SIZE = 512
        D_FF = 4 * HIDDEN_SIZE
        BATCH, SEQ = (2, 256)
        key = jax.random.key(seed)
        k0, k1, k2, k3, k4 = jax.random.split(key, 5)
        scale = 0.02
        return {'hidden_states': jax.random.normal(k0, (BATCH, SEQ, HIDDEN_SIZE), dtype=jnp.float32), 'W1': jax.random.normal(k1, (HIDDEN_SIZE, D_FF), dtype=jnp.float32) * scale, 'fc1_bias': jax.random.normal(k2, (D_FF,), dtype=jnp.float32) * scale, 'W2': jax.random.normal(k3, (D_FF, HIDDEN_SIZE), dtype=jnp.float32) * scale, 'fc2_bias': jax.random.normal(k4, (HIDDEN_SIZE,), dtype=jnp.float32) * scale}
    _L0_ffn_in = _L0_ffn_setup()

    def _L1_attn_setup():
        import jax, jax.numpy as jnp
        import numpy as np
        HIDDEN = 512
        N_HEADS = 32
        N_KV = 8
        HEAD_DIM = HIDDEN // N_HEADS
        Q_PER_KV = N_HEADS // N_KV
        SEQ = 256
        ROPE_BASE = 1000000.0
        POS_SCALE = 1.0
        SM_SCALE = 1.0 / HEAD_DIM
        BLOCK = 64
        LOCAL_BLOCKS = 16
        VERT_STRIDE = 8

        def _blocksparse_mask(seq_len):
            nb = seq_len // BLOCK
            qb = np.arange(nb)[:, None]
            kb = np.arange(nb)[None, :]
            bmask = (kb <= qb) & ((qb - kb < LOCAL_BLOCKS) | ((kb + 1) % VERT_STRIDE == 0))
            emask = np.kron(bmask, np.ones((BLOCK, BLOCK), dtype=bool))
            i = np.arange(seq_len)
            emask &= i[:, None] >= i[None, :]
            return jnp.asarray(emask)

        def _rope(x, cos, sin):
            x1, x2 = jnp.split(x, 2, axis=-1)
            rot = jnp.concatenate([-x2, x1], axis=-1)
            return x * cos[None, :, None, :] + rot * sin[None, :, None, :]
        key = jax.random.key(seed)
        k1, k2, k3, k4, k5 = jax.random.split(key, 5)
        qkv_out = (N_HEADS + 2 * N_KV) * HEAD_DIM
        return {'hidden_states': jax.random.normal(k1, (1, SEQ, HIDDEN), dtype=jnp.float32), 'w_qkv': jax.random.normal(k2, (qkv_out, HIDDEN), dtype=jnp.float32) * 0.02, 'b_qkv': jnp.zeros((qkv_out,), dtype=jnp.float32), 'w_dense': jax.random.normal(k3, (HIDDEN, HIDDEN), dtype=jnp.float32) * 0.02, 'b_dense': jnp.zeros((HIDDEN,), dtype=jnp.float32)}
    _L1_attn_in = _L1_attn_setup()

    def _L1_ffn_setup():
        import jax, jax.numpy as jnp
        import numpy as np
        M = 512
        K = 512

        def _make_2to4_mask(key, shape):
            scores = jax.random.normal(key, shape)
            g = scores.reshape(shape[0], shape[1] // 4, 4)
            rank = jnp.argsort(jnp.argsort(-jnp.abs(g), axis=-1), axis=-1)
            return (rank < 2).reshape(shape).astype(jnp.float32)
        key = jax.random.key(seed)
        k_x, k_w12, k_b12, k_w3, k_b3, k_m = jax.random.split(key, 6)
        x = jax.random.normal(k_x, (4, 256, K), dtype=jnp.float32)
        w12_dense = jax.random.normal(k_w12, (2 * M, K), dtype=jnp.float32) * (1.0 / np.sqrt(K))
        mask12 = _make_2to4_mask(k_m, (2 * M, K))
        w12 = w12_dense * mask12
        b12 = jax.random.normal(k_b12, (2 * M,), dtype=jnp.float32) * 0.01
        w3 = jax.random.normal(k_w3, (M, M), dtype=jnp.float32) * (1.0 / np.sqrt(M))
        b3 = jax.random.normal(k_b3, (M,), dtype=jnp.float32) * 0.01
        return {'x': x, 'w12': w12, 'b12': b12, 'w3': w3, 'b3': b3}
    _L1_ffn_in = _L1_ffn_setup()
    _d = {'L0_attn_x': _L0_attn_in['x'], 'L0_attn_Wq': _L0_attn_in['Wq'], 'L0_attn_Wk': _L0_attn_in['Wk'], 'L0_attn_Wv': _L0_attn_in['Wv'], 'L0_attn_Wo': _L0_attn_in['Wo'], 'L0_ffn_W1': _L0_ffn_in['W1'], 'L0_ffn_fc1_bias': _L0_ffn_in['fc1_bias'], 'L0_ffn_W2': _L0_ffn_in['W2'], 'L0_ffn_fc2_bias': _L0_ffn_in['fc2_bias'], 'L1_attn_w_qkv': _L1_attn_in['w_qkv'], 'L1_attn_b_qkv': _L1_attn_in['b_qkv'], 'L1_attn_w_dense': _L1_attn_in['w_dense'], 'L1_attn_b_dense': _L1_attn_in['b_dense'], 'L1_ffn_w12': _L1_ffn_in['w12'], 'L1_ffn_b12': _L1_ffn_in['b12'], 'L1_ffn_w3': _L1_ffn_in['w3'], 'L1_ffn_b3': _L1_ffn_in['b3']}
    _x0 = _d['L0_attn_x']
    _d['L0_attn_x'] = jax.random.normal(jax.random.fold_in(jax.random.key(seed), 1), (4, 256, 512), dtype=_x0.dtype)
    del _x0
    return _d

def reference(L0_attn_x, L0_attn_Wq, L0_attn_Wk, L0_attn_Wv, L0_attn_Wo, L0_ffn_W1, L0_ffn_fc1_bias, L0_ffn_W2, L0_ffn_fc2_bias, L1_attn_w_qkv, L1_attn_b_qkv, L1_attn_w_dense, L1_attn_b_dense, L1_ffn_w12, L1_ffn_b12, L1_ffn_w3, L1_ffn_b3):

    def _L0_attn_ref(x, Wq, Wk, Wv, Wo):
        import jax, jax.numpy as jnp
        import numpy as np
        EMBED = 512
        NUM_Q_HEADS = 32
        NUM_KV_HEADS = 8
        HEAD_DIM = EMBED // NUM_Q_HEADS
        N_REP = 4
        B, T, C = x.shape
        q = (x @ Wq.T).reshape(B, T, NUM_Q_HEADS, HEAD_DIM).transpose(0, 2, 1, 3)
        k = (x @ Wk.T).reshape(B, T, NUM_KV_HEADS, HEAD_DIM).transpose(0, 2, 1, 3)
        v = (x @ Wv.T).reshape(B, T, NUM_KV_HEADS, HEAD_DIM).transpose(0, 2, 1, 3)
        k = jnp.repeat(k, N_REP, axis=1)
        v = jnp.repeat(v, N_REP, axis=1)
        scale = 1.0 / np.sqrt(HEAD_DIM).astype(np.float32)
        attn = jnp.einsum('bhqd,bhkd->bhqk', q, k) * scale
        attn = jax.nn.softmax(attn, axis=-1)
        out = jnp.einsum('bhqk,bhkd->bhqd', attn, v)
        out = out.transpose(0, 2, 1, 3).reshape(B, T, C)
        return out @ Wo.T

    def _L0_ffn_ref(hidden_states, W1, fc1_bias, W2, fc2_bias):
        import jax, jax.numpy as jnp
        import numpy as np
        HIDDEN_SIZE = 512
        D_FF = 4 * HIDDEN_SIZE
        BATCH, SEQ = (2, 256)
        orig_shape = hidden_states.shape
        x = hidden_states.astype(jnp.float32).reshape(-1, HIDDEN_SIZE)
        h = jax.nn.gelu(x @ W1 + fc1_bias)
        out = (h @ W2).reshape(orig_shape).astype(hidden_states.dtype)
        return out + fc2_bias

    def _L1_attn_ref(hidden_states, w_qkv, b_qkv, w_dense, b_dense):
        import jax, jax.numpy as jnp
        import numpy as np
        HIDDEN = 512
        N_HEADS = 32
        N_KV = 8
        HEAD_DIM = HIDDEN // N_HEADS
        Q_PER_KV = N_HEADS // N_KV
        SEQ = 256
        ROPE_BASE = 1000000.0
        POS_SCALE = 1.0
        SM_SCALE = 1.0 / HEAD_DIM
        BLOCK = 64
        LOCAL_BLOCKS = 16
        VERT_STRIDE = 8

        def _blocksparse_mask(seq_len):
            nb = seq_len // BLOCK
            qb = np.arange(nb)[:, None]
            kb = np.arange(nb)[None, :]
            bmask = (kb <= qb) & ((qb - kb < LOCAL_BLOCKS) | ((kb + 1) % VERT_STRIDE == 0))
            emask = np.kron(bmask, np.ones((BLOCK, BLOCK), dtype=bool))
            i = np.arange(seq_len)
            emask &= i[:, None] >= i[None, :]
            return jnp.asarray(emask)

        def _rope(x, cos, sin):
            x1, x2 = jnp.split(x, 2, axis=-1)
            rot = jnp.concatenate([-x2, x1], axis=-1)
            return x * cos[None, :, None, :] + rot * sin[None, :, None, :]
        B, S, _ = hidden_states.shape
        qkv = jnp.einsum('bsh,oh->bso', hidden_states, w_qkv) + b_qkv
        qkv = qkv.reshape(B, S, N_KV, Q_PER_KV + 2, HEAD_DIM)
        q = qkv[:, :, :, :Q_PER_KV].reshape(B, S, N_HEADS, HEAD_DIM)
        k = qkv[:, :, :, Q_PER_KV]
        v = qkv[:, :, :, Q_PER_KV + 1]
        inv_freq = 1.0 / ROPE_BASE ** (jnp.arange(0, HEAD_DIM, 2, dtype=jnp.float32) / HEAD_DIM)
        t = jnp.arange(S, dtype=jnp.float32) * POS_SCALE
        freqs = jnp.outer(t, inv_freq)
        emb = jnp.concatenate([freqs, freqs], axis=-1)
        cos, sin = (jnp.cos(emb), jnp.sin(emb))
        q = _rope(q, cos, sin)
        k = _rope(k, cos, sin)
        k = jnp.repeat(k, Q_PER_KV, axis=2)
        v = jnp.repeat(v, Q_PER_KV, axis=2)
        mask = _blocksparse_mask(S)
        scores = jnp.einsum('bqhd,bkhd->bhqk', q, k) * SM_SCALE
        scores = jnp.where(mask[None, None], scores, jnp.finfo(scores.dtype).min)
        probs = jax.nn.softmax(scores, axis=-1)
        ctx = jnp.einsum('bhqk,bkhd->bqhd', probs, v).reshape(B, S, HIDDEN)
        out = jnp.einsum('bsh,oh->bso', ctx, w_dense) + b_dense
        return out

    def _L1_ffn_ref(x, w12, b12, w3, b3):
        import jax, jax.numpy as jnp
        import numpy as np
        M = 512
        K = 512

        def _make_2to4_mask(key, shape):
            scores = jax.random.normal(key, shape)
            g = scores.reshape(shape[0], shape[1] // 4, 4)
            rank = jnp.argsort(jnp.argsort(-jnp.abs(g), axis=-1), axis=-1)
            return (rank < 2).reshape(shape).astype(jnp.float32)
        x12 = jnp.einsum('bsk,mk->bsm', x, w12) + b12
        x1, x2 = jnp.split(x12, 2, axis=-1)
        x4 = jax.nn.silu(x1) * x2
        return jnp.einsum('bsm,nm->bsn', x4, w3) + b3
    x = L0_attn_x
    xn = _layernorm(x, axis=-1)
    x = x + _L0_attn_ref(xn, L0_attn_Wq, L0_attn_Wk, L0_attn_Wv, L0_attn_Wo) + _L0_ffn_ref(xn, L0_ffn_W1, L0_ffn_fc1_bias, L0_ffn_W2, L0_ffn_fc2_bias)
    xn = _layernorm(x, axis=-1)
    x = x + _L1_attn_ref(xn, L1_attn_w_qkv, L1_attn_b_qkv, L1_attn_w_dense, L1_attn_b_dense) + _L1_ffn_ref(xn, L1_ffn_w12, L1_ffn_b12, L1_ffn_w3, L1_ffn_b3)
    return x

_drawn_inputs = setup_inputs


def setup_inputs(seed=0):
    import zlib

    import numpy as np

    out = dict(_drawn_inputs(seed))
    spreads = {'L1_attn_b_qkv': (0.0, 0.1), 'L1_attn_b_dense': (0.0, 0.1)}
    factors = {'L0_ffn_fc1_bias': 5.357, 'L0_ffn_fc2_bias': 2.883, 'L1_ffn_b12': 8.0, 'L1_ffn_b3': 6.458}
    for name, (base, spread) in spreads.items():
        noise = np.random.default_rng([zlib.crc32(name.encode()), seed]).standard_normal(out[name].shape)
        drawn = base * np.exp(spread * noise) if base else spread * noise
        out[name] = jnp.asarray(drawn.astype(out[name].dtype))
    for name, factor in factors.items():
        out[name] = (out[name] * factor).astype(out[name].dtype)
    return out
```

```python
from contextlib import ExitStack

import numpy as np

import concourse.bass as bass
from concourse import mybir

F32 = mybir.dt.float32
F32R = mybir.dt.float32r
BF16 = mybir.dt.bfloat16
ALU = mybir.AluOpType
ACT = mybir.ActivationFunctionType
AX = mybir.AxisListType

P = 128
B, T, D = 4, 256, 512
HD = 16
NH, NKV = 32, 8
REP = NH // NKV
KT = D // P
QKV = (NH + 2 * NKV) * HD
S = 4
UH = NH // S
TT = T // P
NT = B * TT
HALF = B * T // 2
HT = HALF // P
ROWS = 96
MROW = 4 * HD
EPS = 1e-5
SCALES = (1.0 / 4.0, 1.0 / 16.0)
MASKED = -1e38
CHUNKS = (2048 // P, 512 // P)
ACC = (0, 1, 2, 6)
HID = (3, 4, 5, 7)


def attention_order(L):
    n0, u0, u1 = B * L, B * S * L, B * S * (L + 1)
    o = [("ln", n0), ("xn", n0, 0), ("xn", n0, 1), ("store_xn", n0)]
    for pair in (2, 0, 1):
        o += [("qkv", n0, pair), ("store", n0, pair)]
    o += [("ln", n0 + 1)]
    o += [("load_km", n0, 0), ("load_q", n0, 0), ("load_q", n0, 1), ("load_km", n0, 1),
          ("load_q", n0, 2), ("load_ke", n0, 0), ("load_ke", n0, 1), ("load_q", n0, 3)]
    for u in (u0, u0 + 1):
        o += [("m", u, i) for i in range(8)]
        if u == u0:
            o += [("mt", u), ("mrow", u)]
    for u in range(u0, u1):
        n, s = divmod(u, S)
        b = n - n0
        for i in range(8):
            if i == 0:
                if s == 0 and b > 0:
                    o += [("load_ke", n, 1), ("load_q", n, 3)]
                if s > 0 and b < B - 1:
                    o += [("load_q", n + 1, s - 1)]
                if s == 1 and b < B - 1:
                    o += [("load_km", n + 1, 0)]
                if s == 2 and b < B - 1:
                    o += [("load_km", n + 1, 1), ("load_ke", n + 1, 0)]
            o += [("st", u, i)]
            if u + 2 < u1:
                o += [("m", u + 2, i)]
            if s == 0 and b < B - 1:
                if i == 0:
                    o += [("xn", n + 1, 0)]
                if i == 1:
                    o += [("xn", n + 1, 1), ("store_xn", n + 1)]
            if i == 1 and u > u0:
                o += [("pv", u - 1, 1)]
            if i == 2 and s == 0:
                o += [("v", n)]
            if i == 2 and u + 1 < u1:
                o += [("mt", u + 1), ("mrow", u + 1)]
            if i in (2, 3, 4, 5) and u > u0:
                o += [("norm", u - 1, i - 2)]
            if s == 0 and b < B - 1 and i == 3:
                o += [("qkv", n + 1, 2), ("store", n + 1, 2)]
            if i == 5:
                o += [("pv", u, 0)]
            if s == 0 and b < B - 1 and i == 5:
                o += [("qkv", n + 1, 0), ("store", n + 1, 0)]
            if s == 1 and b < B - 1 and i == 1:
                o += [("qkv", n + 1, 1), ("store", n + 1, 1)]
            if s == 0 and b > 0 and i in (6, 7):
                o += [("wo", n - 1, i - 6)]
            if s == 2 and i == 4 and b + 2 < B:
                o += [("ln", n + 2)]
            if b == B - 1 and s == 2 and i == 0:
                o += [("load_xf", L, 0)]
            if b == B - 1 and s == 2 and i in (3, 5, 7):
                o += [("split", L, "up", 0) if i == 3 else ("split", L, "up", 1) if i == 5 else ("split", L, "down", 0)]
    o += [("load_xf", L, 1), ("pv", u1 - 1, 1)]
    o += [("norm", u1 - 1, k) for k in range(4)]
    o += [("wo", n0 + B - 1, 0), ("wo", n0 + B - 1, 1)]
    return o


def ffn_order(L):
    C = CHUNKS[L]
    o = []
    for c in range(2 * C + 1):
        if c < 2 * C:
            o += [("up", L, c)]
            if c + 2 < 2 * C:
                o += [("split", L, "up", c + 2)]
            if c + 1 < 2 * C:
                o += [("split", L, "down", c + 1)]
        if c >= 1:
            if (c - 1) % C == 0:
                o += [("bias", L, (c - 1) // C)]
            o += [("down", L, c - 1)]
            if (c - 1) % C == C - 1:
                h = (c - 1) // C
                o += [("add", L, h)]
                o += [("stats", 1, h)] if L == 0 else [("out", h)]
        if L == 0 and c == 2 * C - 1:
            o += [("split", 1, "attn", k) for k in range(4)]
    return o


def program_order():
    o = [("split", 0, "attn", k) for k in range(4)] + [("stats", 0, 0), ("stats", 0, 1)]
    for L in range(2):
        o += attention_order(L) + ffn_order(L)
    return o


def numbered(order, *kinds):
    return {x: k for k, x in enumerate(x for x in order if x[0] in kinds)}


def build(nc, x_in, attn_w, up_w, down_w, up_b, qkv_b, out_b, rope, out):
    order = program_order()
    wk = numbered(order, "m", "mt", "xn", "qkv", "v", "wo")
    cp = numbered(order, "xn", "qkv")
    sp = numbered(order, "split")
    stg = numbered(order, "store")
    stt = numbered(order, "stats")
    lns = numbered(order, "ln")
    ups = numbered(order, "up")
    downs = numbered(order, "down")
    adds = numbered(order, "add")
    hips = {x: k for k, x in enumerate(x for x in order if x[0] == "qkv" and x[1] >= B)}

    qscr = nc.dram_tensor("q_parts", (2 * B, S, 2 * HD, UH * T), F32, kind="Internal").ap()
    kscr = nc.dram_tensor("k_parts", (2 * B, 4, HD, NKV * T), F32, kind="Internal").ap()
    xscr = nc.dram_tensor("xn_parts", (2, 2, P, 2 * KT, HALF), F32, kind="Internal").ap()

    with ExitStack() as ctx:
        def sb(name, shape, dt=F32):
            return ctx.enter_context(nc.sbuf_tensor(name, shape, dt))

        def sem(name):
            return ctx.enter_context(nc.semaphore(name))

        banks = ctx.enter_context(nc.psum_tensor("banks", [P, 8, 512], F32))
        x_res = sb("x_res", [P, NT, D])
        w_qkv = sb("w_qkv", [P, 2, KT, QKV], F32R)
        w_out = sb("w_out", [P, 2, S, D], F32R)
        raw = sb("raw", [P, 2, 1536])
        w_up = sb("w_up", [P, 2, 2, 1024], F32R)
        w_down = sb("w_down", [P, 2, 2, 512], F32R)
        xn = sb("xn", [P, TT, D])
        xnT = sb("xnT", [P, 2, KT, T], F32R)
        big = sb("big", [P, S, UH, T], F32R)
        k_max = sb("k_max", [ROWS, NKV, T], F32R)
        k_exp = sb("k_exp", [ROWS, NKV, T], F32R)
        v_t = sb("v_t", [P, T])
        v_sb = sb("v_sb", [P, TT, NKV, 2 * HD])
        stage = sb("stage", [P, 2, 2, 2, T], F32R)
        probs = sb("probs", [P, 8, 512])
        neg_max = sb("neg_max", [P, S, TT, UH])
        max_t = sb("max_t", [UH, 2, T], F32R)
        o_tok = sb("o_tok", [P, 2 * T])
        o_rec = sb("o_rec", [P, 16])
        o_div = sb("o_div", [P, T])
        o_t = sb("o_t", [P, T])
        ctxT = sb("ctxT", [P, 2, S, T], F32R)
        qkv_v = sb("qkv_v", [P, 2, T])
        rot_a = sb("rot_a", [P, 2, T])
        rot_b = sb("rot_b", [P, 2, T])
        table = sb("table", [P, 2, T])
        bias_qkv = sb("bias_qkv", [P, QKV // P])
        bias_up = sb("bias_up", [P, 24])
        bias_out = sb("bias_out", [P, 2, D], F32R)
        ones = sb("ones", [P, P], F32R)
        ident = sb("ident", [P, P])
        identb = sb("identb", [P, P], BF16)
        mask_qk = sb("mask_qk", [P, P], BF16)
        mask_kq = sb("mask_kq", [P, P], BF16)
        bn = sb("bn", [P, NT, 6])
        mv = sb("mv", [P, NT, 2])
        var_e = sb("var_e", [P, NT])
        dev = sb("dev", [P, NT])
        rs0 = sb("rs0", [P, NT])
        rs1 = sb("rs1", [P, NT])
        rstd = sb("rstd", [P, NT])

        hid = probs[:, :, :].rearrange("p (k s) t -> p k s t", k=4)
        hid_hi, hid_lo = (stage[:, :, e, :, :].rearrange("p k j t -> p k (j t)") for e in range(2))
        bias_raw = probs[:, 0:2, :]
        hid_f = hid[:, 0]
        gate_f = hid[:, 1]

        x_loaded = [sem(f"x_loaded{b}") for b in range(B)]
        c_loaded = sem("c_loaded")
        made = sem("made")
        bias_split = sem("bias_split")
        raw_loaded = [sem(f"raw_loaded{k}") for k in range(2)]
        hi_split = sem("hi_split")
        lo_split = sem("lo_split")
        var_ready = sem("var_ready")
        dev_ready = sem("dev_ready")
        stat_steps = sem("stat_steps")
        ln_done = sem("ln_done")
        wk_filled = sem("wk_filled")
        wk_copied = sem("wk_copied")
        wk_emptied = sem("wk_emptied")
        xn_stored = sem("xn_stored")
        staged = [sem(f"staged{k}") for k in range(2)]
        q_loaded = [sem(f"q_loaded{k}") for k in range(S)]
        km_loaded = [sem(f"km_loaded{k}") for k in range(2)]
        ke_loaded = [sem(f"ke_loaded{k}") for k in range(2)]
        m_loaded = [sem(f"m_loaded{k}") for k in range(S)]
        st_filled = sem("st_filled")
        exp_done = sem("exp_done")
        pv_done = sem("pv_done")
        o_turned = sem("o_turned")
        o_inverted = sem("o_inverted")
        o_divided = sem("o_divided")
        o_back = sem("o_back")
        ctx_hi = sem("ctx_hi")
        ctx_lo = sem("ctx_lo")
        rot_cos = sem("rot_cos")
        rot_sin = sem("rot_sin")
        rot_done = sem("rot_done")
        rot_hi = sem("rot_hi")
        rot_lo = sem("rot_lo")
        xf_loaded = [sem(f"xf_loaded{k}") for k in range(2)]
        up_done = sem("up_done")
        hi_done = sem("hi_done")
        full_done = sem("full_done")
        gate_done = sem("gate_done")
        lo_done = sem("lo_done")
        bias_added = sem("bias_added")
        down_done = sem("down_done")
        added = sem("added")
        out_done = sem("out_done")

        def st_index(u, i):
            return 8 * u + i

        def unit(u):
            n, s = divmod(u, S)
            return n, s, s // 2

        def stores_in(layers, slot):
            return sum(k % 2 == slot for x, k in stg.items() if x[1] < B * layers)

        def work_bank(x):
            return 3 + wk[x] % 3

        def piece(L, what, k):
            if what == "attn":
                if k < 2:
                    return attn_w[L][:, k * 1536:(k + 1) * 1536], 1536, \
                        [w_qkv[:, h, 2 * k:2 * k + 2, :].rearrange("p k n -> p (k n)") for h in range(2)]
                at = KT * QKV + (k - 2) * 1024
                return attn_w[L][:, at:at + 1024], 1024, \
                    [w_out[:, h, 2 * (k - 2):2 * (k - 2) + 2, :].rearrange("p k n -> p (k n)") for h in range(2)]
            c = k % CHUNKS[L]
            if what == "up":
                n = 512 * (L + 1)
                return up_w[L][c], n, [w_up[:, k % 2, h, 0:n] for h in range(2)]
            return down_w[L][c], 512, [w_down[:, k % 2, h, :] for h in range(2)]

        def wait_weights_free(eng, L, what, k):
            if what == "attn" and L == 1:
                eng.wait_ge(wk_filled, wk[("wo", B - 1, 1)] + 1)
            if what == "up" and ups[("up", L, k)] >= 2:
                eng.wait_ge(up_done, ups[("up", L, k)] - 1)
            if what == "down" and downs[("down", L, k)] >= 2:
                eng.wait_ge(down_done, downs[("down", L, k)] - 1)

        block = ctx.enter_context(nc.Block())

        @block.sync
        def _(sp_):
            for b in range(B):
                sp_.dma_start(x_res[:, TT * b:TT * b + TT, :],
                              x_in[b].rearrange("(t p) d -> p t d", p=P)).then_inc(x_loaded[b], 16)
                if b == 0:
                    for dst, src in ((table[:, :, :], rope), (bias_qkv[:, :], qkv_b), (bias_up[:, :], up_b)):
                        sp_.dma_start(dst, src).then_inc(c_loaded, 16)
            sp_.wait_ge(made, 1)
            for row in (0, 32):
                sp_.dma_start(bias_raw[row:row + 2, :, :], out_b).then_inc(c_loaded, 16)
            for x in order:
                if x[0] == "store_xn":
                    n = x[1]
                    L, b = divmod(n, B)
                    sp_.wait_ge(wk_emptied, wk[("xn", n, 1)] + 1)
                    if n >= 1:
                        sp_.wait_ge(xn_stored, 16 * n)
                    sp_.dma_start(xscr[L, b // 2, :, :, (b % 2) * T:(b % 2) * T + T],
                                  xnT[:, :, :, :].rearrange("p h k t -> p (h k) t").bitcast(F32)).then_inc(xn_stored, 16)
                if x[0] == "store":
                    _, n, pair = x
                    k = stg[x]
                    if n < B:
                        sp_.wait_ge(wk_emptied, wk[("qkv", n, pair)] + 1)
                    else:
                        sp_.wait_ge(rot_lo, hips[("qkv", n, pair)] + 1)
                    if pair < 2:
                        for j in range(2):
                            dst = qscr[n, 2 * pair + j].rearrange("(h d) (g t) -> (d g) h t", h=2, g=UH)
                            sp_.dma_start(dst, stage[:, k % 2, :, j, :].bitcast(F32)).then_inc(staged[k % 2], 16)
                    else:
                        for j in range(2):
                            dst = kscr[n].rearrange("(h e) d (g t) -> e (d g) h t", e=2, g=NKV)[j]
                            sp_.dma_start(dst, stage[:, k % 2, :, 0, :].bitcast(F32)).then_inc(staged[k % 2], 16)
                if x[0] == "load_q":
                    _, n, s = x
                    k = stg[("store", n, s // 2)]
                    sp_.wait_ge(staged[k % 2], 32 * (k // 2 + 1))
                    if n % B:
                        sp_.wait_ge(st_filled, st_index(S * (n - 1) + s, 7) + 1)
                    elif n:
                        sp_.wait_ge(up_done, ups[("up", 0, (s // 2 + 1) * CHUNKS[0] - 1)] + 1)
                    else:
                        sp_.wait_ge(made, 6)
                    for e in range(2):
                        sp_.dma_start(big[32 * e:32 * e + 32, s, :, :].rearrange("p g t -> p (g t)").bitcast(F32),
                                      qscr[n, s]).then_inc(q_loaded[s], 16)
                if x[0] in ("load_km", "load_ke"):
                    kind, n, f = x
                    k = stg[("store", n, 2)]
                    sp_.wait_ge(staged[k % 2], 32 * (k // 2 + 1))
                    g = slice(4 * f * T, (4 * f + 4) * T)
                    buf, done = (k_max, km_loaded[f]) if kind == "load_km" else (k_exp, ke_loaded[f])
                    if n == 0:
                        sp_.wait_ge(made, 6)
                    elif kind == "load_km":
                        sp_.wait_ge(wk_filled, wk[("m", S * (n - 1) + 2 * f + 1, 7)] + 1)
                    else:
                        sp_.wait_ge(st_filled, st_index(S * (n - 1) + 2 * f + 1, 7) + 1)
                    sp_.dma_start(buf[0:4 * HD, 4 * f:4 * f + 4, :].rearrange("p g t -> p (g t)").bitcast(F32),
                                  kscr[n].rearrange("q d x -> (q d) x")[:, g]).then_inc(done, 16)
                if x[0] == "mrow":
                    u = x[1]
                    n, s, f = unit(u)
                    sp_.wait_ge(wk_emptied, wk[("mt", u)] + 1)
                    sp_.dma_start(big[MROW:MROW + 1, s, :, :].bitcast(F32),
                                  max_t[:, u % 2, :].bitcast(F32)).then_inc(m_loaded[s], 16)
                if x[0] == "load_xf":
                    _, L, h = x
                    sp_.wait_ge(xn_stored, 16 * B * (L + 1))
                    sp_.wait_ge(st_filled, st_index(B * S * L + S * (B - 1) + 2 * h + 1, 7) + 1)
                    for e in range(2):
                        sp_.dma_start(big[64 * e:64 * e + 64, 2 * h:2 * h + 2, :, :].rearrange("p a g t -> p (a g t)").bitcast(F32),
                                      xscr[L, h, 64 * e:64 * e + 64].rearrange("p k t -> p (k t)")).then_inc(xf_loaded[h], 16)
                if x[0] == "out":
                    h = x[1]
                    for t in range(HT):
                        tile = HT * h + t
                        sp_.wait_ge(added, 4 * adds[("add", 1, h)] + t + 1)
                        sp_.dma_start(out[tile // TT, (tile % TT) * P:(tile % TT) * P + P, :],
                                      x_res[:, tile, :]).then_inc(out_done, 16)
            sp_.wait_ge(out_done, 16 * NT)

        @block.gpsimd
        def _(pool):
            def load(k, x):
                src, n, _ = piece(*x[1:])
                pool.dma_start(raw[:, k % 2, 0:n], src).then_inc(raw_loaded[k % 2], 16)

            pieces = [x for x in order if x[0] == "split"]
            load(0, pieces[0])
            load(1, pieces[1])
            nc.gpsimd.memset(bias_raw[:, :, :], 0.0).then_inc(made, 1)
            pool.wait_ge(made, 1)
            nc.gpsimd.memset(ident[:, :], 0.0).then_inc(made, 1)
            pool.wait_ge(made, 2)
            nc.gpsimd.memset(k_max[64:ROWS, :, :].bitcast(F32), 0.0).then_inc(made, 1)
            pool.wait_ge(made, 3)
            nc.gpsimd.memset(big[64:ROWS, :, :, :].bitcast(F32), 0.0).then_inc(made, 1)
            pool.wait_ge(made, 4)
            nc.gpsimd.memset(k_exp[64:ROWS, :, :].bitcast(F32), 0.0).then_inc(made, 1)
            pool.wait_ge(made, 5)
            nc.gpsimd.memset(k_exp[MROW:MROW + 1, :, :].bitcast(F32), 1.0).then_inc(made, 1)
            pool.wait_ge(made, 6)
            nc.gpsimd.affine_select(out=ident[:, :], in_=ident[:, :], compare_op=ALU.not_equal, fill=1.0,
                                    base=0, pattern=[[-1, P]], channel_multiplier=1).then_inc(made, 1)
            pool.wait_ge(made, 7)
            nc.gpsimd.memset(mask_qk[:, :], 0.0).then_inc(made, 1)
            pool.wait_ge(made, 8)
            nc.gpsimd.memset(mask_kq[:, :], 0.0).then_inc(made, 1)
            pool.wait_ge(made, 9)
            nc.gpsimd.memset(v_sb[:, :, :, :], 1.0).then_inc(made, 1)
            pool.wait_ge(made, 10)
            nc.gpsimd.memset(ones[:, :].bitcast(F32), 1.0).then_inc(made, 1)
            pool.wait_ge(made, 11)
            nc.gpsimd.affine_select(out=mask_qk[:, :], in_=mask_qk[:, :], compare_op=ALU.is_ge, fill=MASKED,
                                    base=0, pattern=[[-1, P]], channel_multiplier=1).then_inc(made, 1)
            pool.wait_ge(made, 12)
            nc.gpsimd.affine_select(out=mask_kq[:, :], in_=mask_kq[:, :], compare_op=ALU.is_ge, fill=MASKED,
                                    base=0, pattern=[[1, P]], channel_multiplier=-1).then_inc(made, 1)
            pool.wait_ge(made, 13)
            last = [(made, 13)]

            def in_order():
                pool.wait_ge(*last[0])

            for x in order:
                if x[0] == "split" and sp[x] + 2 < len(pieces):
                    pool.wait_ge(lo_split, sp[x] + 1)
                    load(sp[x] + 2, pieces[sp[x] + 2])
                if x[0] == "norm" and x[2] == 3:
                    u = x[1]
                    n, s, f = unit(u)
                    pool.wait_ge(ctx_hi, u + 1)
                    in_order()
                    nc.gpsimd.tensor_tensor(ctxT[:, 1, s, :], o_t[:, :], ctxT[:, 0, s, :].bitcast(F32),
                                            ALU.subtract).then_inc(ctx_lo, 1)
                    last[0] = (ctx_lo, u + 1)
                if x[0] == "qkv" and x[1] >= B:
                    _, n, pair = x
                    w = 2 if pair < 2 else 1
                    k = stg[("store", n, pair)]
                    pool.wait_ge(wk_copied, cp[x] + 1)
                    if hips[x]:
                        pool.wait_ge(rot_done, hips[x])
                    in_order()
                    nc.gpsimd.tensor_tensor(rot_a[:, 0:w, :], qkv_v[:, 0:w, :],
                                            table[:, 0:1, :].to_broadcast([P, w, T]), ALU.mult).then_inc(rot_cos, 1)
                    last[0] = (rot_cos, hips[x] + 1)
                    pool.wait_ge(rot_hi, hips[x] + 1)
                    in_order()
                    nc.gpsimd.tensor_tensor(stage[:, k % 2, 1, 0:w, :], rot_b[:, 0:w, :],
                                            stage[:, k % 2, 0, 0:w, :].bitcast(F32), ALU.subtract).then_inc(rot_lo, 1)
                    last[0] = (rot_lo, hips[x] + 1)

        @block.tensor
        def _(pe):
            def work(x):
                if wk[x] >= 3:
                    pe.wait_ge(wk_emptied, wk[x] - 2)
                return work_bank(x)

            def three(out_ap, lhs, rhs, first, last, **kw):
                for j, (a, b_) in enumerate(((0, 0), (1, 0), (0, 1))):
                    mm = nc.tensor.matmul(out_ap, lhs(a), rhs(b_), start=first and j == 0, stop=last and j == 2, **kw)
                return mm

            pe.wait_ge(made, 14)
            for x in order:
                if x[0] == "xn":
                    _, n, t = x
                    k = work(x)
                    pe.wait_ge(ln_done, TT * n + t + 1)
                    for c in range(KT):
                        mm = nc.tensor.transpose(banks[:, k, c * P:c * P + P], xn[:, t, c * P:c * P + P], ident[:, :])
                    mm.then_inc(wk_filled, 1)
                if x[0] == "qkv":
                    _, n, pair = x
                    k = work(x)
                    pe.wait_ge(wk_emptied, wk[("xn", n, 1)] + 1)
                    pe.wait_ge(lo_split, sp[("split", n // B, "attn", 1)] + 1)
                    for j in range(2):
                        m = (2 * pair + j) * P
                        for c in range(KT):
                            mm = three(banks[:, k, j * T:j * T + T],
                                       lambda h: w_qkv[:, h, c, m:m + P], lambda h: xnT[:, h, c, :],
                                       c == 0, c == KT - 1)
                    mm.then_inc(wk_filled, 1)
                if x[0] == "v":
                    n = x[1]
                    k = work(x)
                    pe.wait_ge(wk_copied, cp[("qkv", n, 2)] + 1)
                    for t in range(TT):
                        mm = nc.tensor.transpose(banks[:, k, t * P:t * P + P], v_t[:, t * P:t * P + P], ident[:, :])
                    mm.then_inc(wk_filled, 1)
                if x[0] == "m":
                    _, u, i = x
                    n, s, f = unit(u)
                    t, g = divmod(i, 4)
                    k = work(x)
                    if i == 0:
                        pe.wait_ge(q_loaded[s], 32 * (n + 1))
                        pe.wait_ge(km_loaded[f], 16 * (n + 1))
                    for r in range(2):
                        mm = nc.tensor.matmul(banks[:, k, r * T:r * T + T],
                                              big[0:ROWS, s, 2 * g + r, t * P:t * P + P], k_max[0:ROWS, 4 * f + g, :],
                                              start=r == 0, stop=n < B and r == 1, skip_group_check=True)
                    if n >= B:
                        diagonal = banks[:, k, :].rearrange("p (r t) -> p r t", r=2)[:, :, t * P:t * P + P]
                        mm = nc.tensor.matmul(diagonal, identb[:, :], mask_qk[:, None, :].to_broadcast([P, 2, P]),
                                              start=False, stop=True, skip_group_check=True)
                    mm.then_inc(wk_filled, 1)
                if x[0] == "mt":
                    u = x[1]
                    n, s, f = unit(u)
                    k = work(x)
                    pe.wait_ge(wk_emptied, wk[("m", u, 7)] + 1)
                    for t in range(TT):
                        mm = nc.tensor.transpose(banks[0:UH, k, t * P:t * P + P], neg_max[:, s, t, :], ident[:, :])
                    mm.then_inc(wk_filled, 1)
                if x[0] == "st":
                    _, u, i = x
                    n, s, f = unit(u)
                    t, g = divmod(i, 4)
                    k = st_index(u, i)
                    if k >= 3:
                        pe.wait_ge(exp_done, k - 2)
                    if i == 0:
                        pe.wait_ge(m_loaded[s], 16 * (n + 1))
                        pe.wait_ge(ke_loaded[f], 16 * (n + 1))
                    keys = k_exp[0:ROWS, 4 * f + g, t * P:t * P + P]
                    bank = banks[:, k % 3, :].rearrange("p (r t) -> p r t", r=2)
                    if n < B:
                        mm = nc.tensor.matmul(bank, keys, big[0:ROWS, s, 2 * g:2 * g + 2, :], start=True, stop=True)
                    else:
                        q0 = t * P
                        part = bank if t == 0 else banks[:, k % 3, 0:2 * P].rearrange("p (r t) -> p r t", r=2)
                        nc.tensor.matmul(part, keys, big[0:ROWS, s, 2 * g:2 * g + 2, q0:], start=True, stop=False,
                                         skip_group_check=True)
                        mm = nc.tensor.matmul(part[:, :, 0:P], identb[:, :], mask_kq[:, None, :].to_broadcast([P, 2, P]),
                                              start=False, stop=True, skip_group_check=True)
                    mm.then_inc(st_filled, 1)
                if x[0] == "pv":
                    _, u, t = x
                    n, s, f = unit(u)
                    pe.wait_ge(exp_done, st_index(u, 4 * t + 3) + 1)
                    if t == 0 and u >= 2:
                        pe.wait_ge(o_turned, u - 1)
                    if t == 0 and s == 0:
                        pe.wait_ge(wk_emptied, wk[("v", n)] + 1)
                    for g in range(4):
                        o = banks[32 * g:32 * g + 32, 6 + u % 2, :]
                        p_ = probs[:, 4 * t + g, :]
                        if n >= B and t == 1:
                            o = o.rearrange("p (r t) -> p r t", r=2)[:, :, P:2 * P]
                            p_ = p_[:, 0:2 * P].rearrange("p (r t) -> p r t", r=2)
                        mm = nc.tensor.matmul(o, v_sb[:, t, 4 * f + g, :], p_, start=t == 0, stop=t == 1,
                                              skip_group_check=True)
                    mm.then_inc(pv_done, 1)
                if x[0] == "wo":
                    _, n, t = x
                    k = work(x)
                    pe.wait_ge(ctx_lo, S * (n + 1))
                    pe.wait_ge(lo_split, sp[("split", n // B, "attn", 3)] + 1)
                    for s in range(S):
                        mm = three(banks[:, k, :], lambda h: ctxT[:, h, s, t * P:t * P + P],
                                   lambda h: w_out[:, h, s, :], s == 0, s == S - 1)
                    mm.then_inc(wk_filled, 1)
                if x[0] == "up":
                    _, L, c = x
                    h = c // CHUNKS[L]
                    pe.wait_ge(lo_split, sp[("split", L, "up", c)] + 1)
                    if c % CHUNKS[L] == 0:
                        pe.wait_ge(xf_loaded[h], 32 * (L + 1))
                    if c < 2:
                        pe.wait_ge(wk_emptied, wk[("wo", B * (L + 1) - 1, 1)] + 1)
                        pe.wait_ge(o_turned, B * S * (L + 1))
                    else:
                        pe.wait_ge(lo_done, ups[x] - 1)
                    xf = big[:, 2 * h:2 * h + 2, :, :].rearrange("p a g t -> p (a g t)").rearrange(
                        "p (h k t) -> p h k t", h=2, k=KT)
                    for j in range(L + 1):
                        k = HID[c % 2] if L == 0 else HID[2 * (c % 2) + j]
                        for q in range(KT):
                            mm = three(banks[:, k, :],
                                       lambda e: w_up[:, c % 2, e, (j * KT + q) * P:(j * KT + q) * P + P],
                                       lambda e: xf[:, e, q, :], q == 0, q == KT - 1)
                    mm.then_inc(up_done, 1)
                if x[0] == "bias":
                    _, L, h = x
                    if h == 0:
                        pe.wait_ge(exp_done, 8 * B * S * (L + 1))
                    else:
                        pe.wait_ge(added, 4 * (2 * L + h))
                    pe.wait_ge(bias_split, 1)
                    for t in range(HT):
                        nc.tensor.matmul(banks[:, ACC[t], :], ones[:, :], bias_out[:, L, :],
                                         start=True, stop=False, skip_group_check=True)
                if x[0] == "down":
                    _, L, c = x
                    pe.wait_ge(lo_split, sp[("split", L, "down", c)] + 1)
                    pe.wait_ge(lo_done, downs[x] + 1)
                    for t in range(HT):
                        mm = three(banks[:, ACC[t], :], lambda h: (hid_hi, hid_lo)[h][:, c % 2, t * P:t * P + P],
                                   lambda h: w_down[:, c % 2, h, :], False, c % CHUNKS[L] == CHUNKS[L] - 1,
                                   skip_group_check=True)
                    mm.then_inc(down_done, 1)

        @block.scalar
        def _(act):
            copies = 0
            for x in order:
                if x[0] == "split":
                    k = sp[x]
                    _, n, parts = piece(*x[1:])
                    act.wait_ge(raw_loaded[k % 2], 16 * (k // 2 + 1))
                    wait_weights_free(act, *x[1:])
                    nc.scalar.copy(parts[0], raw[:, k % 2, 0:n]).then_inc(hi_split, 1)
                if x[0] == "stats":
                    k = stt[x]
                    t = slice(HT * x[2], HT * x[2] + HT)
                    act.wait_ge(var_ready, k + 1)
                    nc.scalar.activation(dev[:, t], var_e[:, t], ACT.Sqrt).then_inc(dev_ready, 1)
                if x[0] == "xn":
                    _, n, t = x
                    act.wait_ge(wk_filled, wk[x] + 1)
                    if n and t == 0:
                        act.wait_ge(wk_filled, wk[("qkv", n - 1, 1)] + 1)
                        act.wait_ge(xn_stored, 16 * n)
                    nc.scalar.copy(xnT[:, 0, :, t * P:t * P + P],
                                   banks[:, work_bank(x), :].rearrange("p (k t) -> p k t", k=KT)).then_inc(wk_copied, 1)
                if x[0] == "qkv":
                    _, n, pair = x
                    k = stg[("store", n, pair)]
                    w = 2 if pair < 2 else 1
                    bank = banks[:, work_bank(x), :].rearrange("p (j t) -> p j t", j=2)
                    act.wait_ge(wk_filled, wk[x] + 1)
                    if n < B:
                        if k >= 2:
                            act.wait_ge(staged[k % 2], 32 * (k // 2))
                        ins = nc.scalar.copy(stage[:, k % 2, 0, 0:w, :], bank[:, 0:w, :])
                    else:
                        if hips[x]:
                            act.wait_ge(rot_cos, hips[x])
                            act.wait_ge(wk_emptied, wk[next(y for y, k_ in hips.items() if k_ == hips[x] - 1)] + 1)
                        for j in range(w):
                            ins = nc.scalar.activation(qkv_v[:, j, :], bank[:, j, :], ACT.Identity,
                                                       bias=bias_qkv[:, 2 * pair + j:2 * pair + j + 1])
                    if pair == 2:
                        if n % B:
                            act.wait_ge(wk_filled, wk[("v", n - 1)] + 1)
                        elif n:
                            act.wait_ge(wk_filled, wk[("v", n - 1)] + 1)
                        if n < B:
                            ins = nc.scalar.copy(v_t[:, :], bank[:, 1, :])
                        else:
                            ins = nc.scalar.activation(v_t[:, :], bank[:, 1, :], ACT.Identity, bias=bias_qkv[:, 5:6])
                    ins.then_inc(wk_copied, 1)
                    if n >= B:
                        act.wait_ge(rot_done, hips[x] + 1)
                        if n == B and pair == 2:
                            act.wait_ge(down_done, 2 * CHUNKS[0])
                        act.wait_ge(staged[k % 2], 32 * (k // 2))
                        nc.scalar.copy(stage[:, k % 2, 0, 0:w, :], rot_b[:, 0:w, :]).then_inc(rot_hi, 1)
                if x[0] == "st":
                    _, u, i = x
                    n, s, f = unit(u)
                    t = i // 4
                    k = st_index(u, i)
                    act.wait_ge(st_filled, k + 1)
                    if k == 0:
                        act.wait_ge(bias_split, 1)
                    if u:
                        act.wait_ge(pv_done, 2 * (u - 1) + t + 1)
                    w = 2 * P if n >= B and t == 1 else 512
                    nc.scalar.activation(probs[:, i, 0:w], banks[:, k % 3, 0:w], ACT.Exp,
                                         scale=SCALES[n // B]).then_inc(exp_done, 1)
                if x[0] == "norm" and x[2] == 3:
                    u = x[1]
                    n, s, f = unit(u)
                    act.wait_ge(o_back, u + 1)
                    if n and s == 0:
                        act.wait_ge(wk_filled, wk[("wo", n - 1, 1)] + 1)
                    nc.scalar.copy(ctxT[:, 0, s, :], o_t[:, :]).then_inc(ctx_hi, 1)
                if x[0] == "up":
                    _, L, c = x
                    k = ups[x]
                    act.wait_ge(up_done, k + 1)
                    act.wait_ge(c_loaded, 80)
                    cc = c % CHUNKS[L]
                    if c == 0:
                        for e in range(2):
                            act.wait_ge(staged[e], 32 * stores_in(L + 1, e))
                    if L == 0:
                        bias = bias_up[:, cc:cc + 1]
                        if k >= 2:
                            act.wait_ge(down_done, k - 1)
                            act.wait_ge(lo_done, k - 1)
                        nc.scalar.activation(hid_hi[:, c % 2, :], banks[:, HID[c % 2], :], ACT.Gelu_apprx_tanh,
                                             bias=bias).then_inc(hi_done, 1)
                        nc.scalar.activation(hid_f[:, c % 2, :], banks[:, HID[c % 2], :], ACT.Gelu_apprx_tanh,
                                             bias=bias).then_inc(full_done, 1)
                    else:
                        act.wait_ge(lo_done, k - 1)
                        nc.scalar.activation(gate_f[:, c % 2, :], banks[:, HID[2 * (c % 2)], :], ACT.Silu,
                                             bias=bias_up[:, 16 + cc:17 + cc]).then_inc(gate_done, 1)
                        act.wait_ge(full_done, k + 1)
                        act.wait_ge(down_done, k - 1)
                        nc.scalar.copy(hid_hi[:, c % 2, :], hid_f[:, c % 2, :]).then_inc(hi_done, 1)

        @block.vector
        def _(dve):
            steps = [0]

            def link(ins):
                steps[0] += 1
                ins.then_inc(stat_steps, 1)
                dve.wait_ge(stat_steps, steps[0])

            dve.wait_ge(made, 13)
            nc.vector.tensor_copy(identb[:, :], ident[:, :]).then_inc(made, 1)
            for x in order:
                if x[0] == "split":
                    k = sp[x]
                    _, n, parts = piece(*x[1:])
                    dve.wait_ge(hi_split, k + 1)
                    nc.vector.tensor_tensor(parts[1], raw[:, k % 2, 0:n], parts[0].bitcast(F32),
                                            ALU.subtract).then_inc(lo_split, 1)
                if x[0] == "stats":
                    _, L, h = x
                    k = stt[x]
                    for t in range(HT * h, HT * h + HT):
                        if L == 0:
                            dve.wait_ge(x_loaded[t // TT], 16)
                        else:
                            dve.wait_ge(added, t + 1)
                        ins = nc.vector.bn_stats(bn[:, t, :], x_res[:, t, :])
                        link(ins)
                        ins = nc.vector.bn_aggr(mv[:, t, :], bn[:, t, :])
                    link(ins)
                    t = slice(HT * h, HT * h + HT)
                    nc.vector.tensor_scalar(var_e[:, t], mv[:, t, 1], EPS, None, ALU.add).then_inc(var_ready, 1)
                    dve.wait_ge(dev_ready, k + 1)
                    link(nc.vector.reciprocal(rs0[:, t], dev[:, t]))
                    link(nc.vector.tensor_tensor(rs1[:, t], rs0[:, t], rs0[:, t], ALU.mult))
                    link(nc.vector.tensor_tensor(rs1[:, t], rs1[:, t], var_e[:, t], ALU.mult))
                    link(nc.vector.tensor_scalar(rs1[:, t], rs1[:, t], -0.5, 1.5, ALU.mult, ALU.add))
                    link(nc.vector.tensor_tensor(rstd[:, t], rs0[:, t], rs1[:, t], ALU.mult))
                    if L == 0 and h == 0:
                        dve.wait_ge(c_loaded, 80)
                        link(nc.vector.tensor_copy(bias_out[:, :, :], bias_raw[:, :, :]))
                        nc.vector.tensor_tensor(bias_out[32:64, :, :], bias_raw[32:64, :, :],
                                                bias_out[32:64, :, :].bitcast(F32), ALU.subtract).then_inc(bias_split, 1)
                if x[0] == "ln":
                    n = x[1]
                    for t in range(TT):
                        tile = TT * (n % B) + t
                        if n:
                            dve.wait_ge(wk_filled, wk[("xn", n - 1, t)] + 1)
                        nc.vector.tensor_scalar(xn[:, t, :], x_res[:, tile, :], mv[:, tile, 0:1], rstd[:, tile:tile + 1],
                                                ALU.subtract, ALU.mult).then_inc(ln_done, 1)
                if x[0] == "xn":
                    _, n, t = x
                    dve.wait_ge(wk_copied, cp[x] + 1)
                    nc.vector.tensor_tensor(xnT[:, 1, :, t * P:t * P + P],
                                            banks[:, work_bank(x), :].rearrange("p (k t) -> p k t", k=KT),
                                            xnT[:, 0, :, t * P:t * P + P].bitcast(F32), ALU.subtract).then_inc(wk_emptied, 1)
                if x[0] == "qkv":
                    _, n, pair = x
                    k = stg[("store", n, pair)]
                    w = 2 if pair < 2 else 1
                    dve.wait_ge(wk_copied, cp[x] + 1)
                    if n < B:
                        bank = banks[:, work_bank(x), :].rearrange("p (j t) -> p j t", j=2)
                        nc.vector.tensor_tensor(stage[:, k % 2, 1, 0:w, :], bank[:, 0:w, :],
                                                stage[:, k % 2, 0, 0:w, :].bitcast(F32), ALU.subtract).then_inc(wk_emptied, 1)
                    else:
                        if hips[x]:
                            dve.wait_ge(rot_lo, hips[x])
                        other = table[:, 1:2, :]
                        nc.vector.tensor_tensor(rot_b[0:64, 0:w, :], qkv_v[64:P, 0:w, :],
                                                other[64:P].to_broadcast([64, w, T]), ALU.mult).then_inc(rot_sin, 1)
                        nc.vector.tensor_tensor(rot_b[64:P, 0:w, :], qkv_v[0:64, 0:w, :],
                                                other[0:64].to_broadcast([64, w, T]), ALU.mult).then_inc(wk_emptied, 1)
                        dve.wait_ge(rot_sin, hips[x] + 1)
                        dve.wait_ge(wk_emptied, wk[x] + 1)
                        dve.wait_ge(rot_cos, hips[x] + 1)
                        nc.vector.tensor_tensor(rot_b[:, 0:w, :], rot_b[:, 0:w, :], rot_a[:, 0:w, :],
                                                ALU.add).then_inc(rot_done, 1)
                if x[0] == "v":
                    n = x[1]
                    dve.wait_ge(wk_filled, wk[x] + 1)
                    if n:
                        dve.wait_ge(pv_done, 2 * S * n)
                    nc.vector.tensor_copy(v_sb[:, :, :, 0:HD],
                                          banks[:, work_bank(x), 0:TT * P].rearrange("p (t g d) -> p t g d", t=TT, g=NKV)
                                          ).then_inc(wk_emptied, 1)
                if x[0] == "m":
                    _, u, i = x
                    n, s, f = unit(u)
                    t, g = divmod(i, 4)
                    dve.wait_ge(wk_filled, wk[x] + 1)
                    if n:
                        dve.wait_ge(wk_filled, wk[("mt", u - S)] + 1)
                    w = T if n < B or t == 1 else P
                    nc.vector.tensor_reduce(neg_max[:, s, t, 2 * g:2 * g + 2],
                                            banks[:, work_bank(x), :].rearrange("p (r t) -> p r t", r=2)[:, :, 0:w],
                                            AX.X, ALU.max, negate=True).then_inc(wk_emptied, 1)
                if x[0] == "mt":
                    u = x[1]
                    n, s, f = unit(u)
                    dve.wait_ge(wk_filled, wk[x] + 1)
                    if u >= 2:
                        dve.wait_ge(m_loaded[(u - 2) % S], 16 * ((u - 2) // S + 1))
                    nc.vector.tensor_copy(max_t[:, u % 2, :], banks[0:UH, work_bank(x), 0:T]).then_inc(wk_emptied, 1)
                if x[0] == "norm":
                    _, u, k = x
                    if k == 0:
                        dve.wait_ge(pv_done, 2 * u + 2)
                        if u:
                            dve.wait_ge(o_divided, u)
                        nc.vector.transpose(o_tok[:, :], banks[:, 6 + u % 2, :]).then_inc(o_turned, 1)
                    by = o_tok[:, :].rearrange("p (r q c) -> p r q c", r=2, q=8)
                    if k == 1:
                        dve.wait_ge(o_turned, u + 1)
                        nc.vector.reciprocal(o_rec[:, :].rearrange("p (r q) -> p r q", r=2), by[:, :, :, HD]).then_inc(o_inverted, 1)
                    if k == 2:
                        dve.wait_ge(o_inverted, u + 1)
                        if u:
                            dve.wait_ge(o_back, u)
                        nc.vector.tensor_tensor(o_div[:, :].rearrange("p (q r c) -> p r q c", r=2, c=HD), by[:, :, :, 0:HD],
                                                o_rec[:, :].rearrange("p (r q a) -> p r q a", r=2, a=1).to_broadcast([P, 2, 8, HD]),
                                                ALU.mult).then_inc(o_divided, 1)
                    if k == 3:
                        dve.wait_ge(o_divided, u + 1)
                        if u:
                            dve.wait_ge(ctx_lo, u)
                        nc.vector.transpose(o_t[:, :], o_div[:, :]).then_inc(o_back, 1)
                if x[0] == "wo":
                    _, n, t = x
                    tile = TT * (n % B) + t
                    dve.wait_ge(wk_filled, wk[x] + 1)
                    nc.vector.tensor_tensor(x_res[:, tile, :], x_res[:, tile, :], banks[:, work_bank(x), :],
                                            ALU.add).then_inc(wk_emptied, 1)
                if x[0] == "up":
                    _, L, c = x
                    k = ups[x]
                    cc = c % CHUNKS[L]
                    if L == 1:
                        dve.wait_ge(gate_done, k - 2 * CHUNKS[0] + 1)
                        nc.vector.scalar_tensor_tensor(out=hid_f[:, c % 2, :], in0=banks[:, HID[2 * (c % 2) + 1], :],
                                                       scalar=bias_up[:, 20 + cc:21 + cc], in1=gate_f[:, c % 2, :],
                                                       op0=ALU.add, op1=ALU.mult).then_inc(full_done, 1)
                    dve.wait_ge(hi_done, k + 1)
                    dve.wait_ge(full_done, k + 1)
                    if k >= 2:
                        dve.wait_ge(down_done, k - 1)
                    nc.vector.tensor_tensor(hid_lo[:, c % 2, :], hid_f[:, c % 2, :], hid_hi[:, c % 2, :].bitcast(F32),
                                            ALU.subtract).then_inc(lo_done, 1)
                if x[0] == "add":
                    _, L, h = x
                    dve.wait_ge(down_done, downs[("down", L, (h + 1) * CHUNKS[L] - 1)] + 1)
                    for t in range(HT):
                        nc.vector.tensor_tensor(x_res[:, HT * h + t, :], x_res[:, HT * h + t, :], banks[:, ACC[t], :],
                                                ALU.add).then_inc(added, 1)


_PERM_HEAD = [[4 * (4 * (s // 2) + g) + 2 * (s % 2) + r for g in range(4) for r in range(2)] for s in range(S)]


def _layouts(i):
    def q_rows(head_row):
        return np.array([head_row(_PERM_HEAD[s][h]) + d for s in range(S) for d in range(HD) for h in range(UH)])

    def kd(base):
        return np.array([base(g) + d for d in range(HD) for g in range(NKV)])

    def gd(base):
        return np.array([base(g) + d for g in range(NKV) for d in range(HD)])

    def by_part(w):
        return w.T.reshape(KT, P, -1).transpose(1, 0, 2)

    block = (REP + 2) * HD
    w0 = np.concatenate([i["L0_attn_Wq"][q_rows(lambda h: h * HD)], i["L0_attn_Wk"][kd(lambda g: g * HD)],
                         i["L0_attn_Wv"][gd(lambda g: g * HD)]])
    rows1 = np.concatenate([q_rows(lambda h: (h // REP) * block + (h % REP) * HD),
                            kd(lambda g: g * block + REP * HD), gd(lambda g: g * block + (REP + 1) * HD)])
    w1 = i["L1_attn_w_qkv"][rows1]
    cols = np.array([_PERM_HEAD[s][h] * HD + d for s in range(S) for h in range(UH) for d in range(HD)])
    outs = [by_part(w[:, cols]) for w in (i["L0_attn_Wo"], i["L1_attn_w_dense"])]
    attn = [np.concatenate([by_part(w).reshape(P, -1), o.reshape(P, -1)], 1) for w, o in zip((w0, w1), outs)]
    up0 = i["L0_ffn_W1"].reshape(KT, P, CHUNKS[0], P).transpose(2, 1, 0, 3).reshape(CHUNKS[0], P, -1)
    up1 = i["L1_ffn_w12"].reshape(2, CHUNKS[1], P, KT, P).transpose(1, 4, 0, 3, 2).reshape(CHUNKS[1], P, -1)
    down0 = i["L0_ffn_W2"].reshape(CHUNKS[0], P, D)
    down1 = i["L1_ffn_w3"].T.reshape(CHUNKS[1], P, D)
    up_b = np.concatenate([i["L0_ffn_fc1_bias"].reshape(-1, P), i["L1_ffn_b12"].reshape(-1, P)]).T
    zero = np.zeros(D, np.float32)
    out_b = np.stack([np.stack([i["L0_ffn_fc2_bias"], i["L1_ffn_b3"]]), np.stack([zero, i["L1_attn_b_dense"]])])
    inv = (np.float32(1.0) / np.power(np.float32(1e6), np.arange(0, HD, 2, dtype=np.float32) / np.float32(HD))).astype(np.float32)
    ang = np.outer(inv, np.arange(T, dtype=np.float32)).astype(np.float32)
    cos, sin = np.cos(ang), np.sin(ang)
    row = np.arange(P) // 8
    rope = np.stack([cos[row % 8], np.where((row < 8)[:, None], sin[row % 8], -sin[row % 8])], 1).astype(np.float32)
    c = np.ascontiguousarray
    return {"x": c(i["L0_attn_x"]), "attn0": c(attn[0]), "attn1": c(attn[1]), "up0": c(up0), "up1": c(up1),
            "down0": c(down0), "down1": c(down1), "up_b": c(up_b), "qkv_b": c(i["L1_attn_b_qkv"][rows1].reshape(-1, P).T),
            "out_b": c(out_b), "rope": c(rope)}


def kernel(**inputs):
    import concourse.bacc as _bacc
    from concourse.bass_utils import run_bass_kernel_spmd as _run

    nc = _bacc.Bacc("TRN2", target_bir_lowering=False, num_devices=1)
    arrays = _layouts({k: np.asarray(v) for k, v in inputs.items()})
    a = {k: nc.dram_tensor(f"in_{k}", v.shape, F32, kind="ExternalInput").ap() for k, v in arrays.items()}
    out = nc.dram_tensor("out", (B, T, D), F32, kind="ExternalOutput").ap()
    build(nc, a["x"], [a["attn0"], a["attn1"]], [a["up0"], a["up1"]], [a["down0"], a["down1"]],
          a["up_b"], a["qkv_b"], a["out_b"], a["rope"], out)
    r = _run(nc, [{f"in_{k}": v for k, v in arrays.items()}], core_ids=[0])
    return r.results[0]["out"]
```

```python
from contextlib import ExitStack

import numpy as np

import concourse.bass as bass
from concourse import mybir

F32 = mybir.dt.float32
F32R = mybir.dt.float32r
BF16 = mybir.dt.bfloat16
ALU = mybir.AluOpType
ACT = mybir.ActivationFunctionType
AX = mybir.AxisListType

P = 128
B, T, D = 4, 256, 512
HD = 16
NH, NKV = 32, 8
REP = NH // NKV
KT = D // P
QKV = (NH + 2 * NKV) * HD
S = 4
UH = NH // S
TT = T // P
NT = B * TT
HALF = B * T // 2
HT = HALF // P
ROWS = 96
MROW = 4 * HD
EPS = 1e-5
SCALES = (1.0 / 4.0, 1.0 / 16.0)
MASKED = -1e38
CHUNKS = (2048 // P, 512 // P)
ACC = (0, 1, 2, 6)
HID = (5, 4, 3, 7)


def attention_start(L):
    n0, u0 = B * L, B * S * L
    o = [("ln", n0), ("xn", n0, 0), ("xn", n0, 1), ("store_xn", n0)]
    for pair in (2, 0):
        o += [("qkv", n0, pair), ("store", n0, pair)]
    o += [("load_km", n0, 0), ("load_q", n0, 0), ("load_q", n0, 1),
          ("qkv", n0, 1), ("store", n0, 1), ("load_ke", n0, 0),
          ("stats", L, 1), ("ln", n0 + 1), ("stats", L, 2), ("v", n0), ("xn", n0 + 1, 0), ("xn", n0 + 1, 1), ("store_xn", n0 + 1),
          ("stats", L, 3), ("load_km", n0, 1), ("load_ke", n0, 1)]
    for pair, u in ((0, u0), (1, u0 + 1)):
        o += [("qkv", n0 + 1, pair), ("store", n0 + 1, pair)]
        o += [("m", u, i) for i in range(8)]
    k = o.index(("m", u0 + 1, 3))
    o = o[:k] + [("mt", u0), ("mrow", u0)] + o[k:] + [("load_q", n0, 2), ("load_q", n0, 3)]
    return [x for x in o if x[0] != "stats" or L == 0]


def attention_order(L):
    n0, u0, u1 = B * L, B * S * L, B * S * (L + 1)
    o = []
    for u in range(u0, u1):
        n, s = divmod(u, S)
        b = n - n0
        more = b < B - 1
        for i in range(8):
            if i == 0:
                if s == 0 and b > 0:
                    o += [("load_ke", n, 1), ("load_q", n, 3)]
                if s > 1 and more:
                    o += [("load_q", n + 1, s - 1)]
                if s == 2 and more:
                    o += [("load_km", n + 1, 1), ("load_ke", n + 1, 0)]
                if s > 0 and not more:
                    o += [("load_xf", L, s - 1)]
            o += [("st", u, i)]
            if u + 2 < u1:
                o += [("m", u + 2, i)]
            if i == 1 and u > u0:
                o += [("pv", u - 1, 1)]
            if i == 2 and s == 0 and b > 0:
                o += [("v", n)]
            if i == 2 and u + 1 < u1:
                o += [("mt", u + 1), ("mrow", u + 1)]
            if i == 3 and s == 1 and more:
                o += [("load_km", n + 1, 0), ("load_q", n + 1, 0)]
            if i in (2, 3, 4, 5) and u > u0:
                o += [("norm", u - 1, i - 2)]
            if i == 5:
                o += [("pv", u, 0)]
            if more and (s, i) == (0, 3):
                o += [("qkv", n + 1, 2), ("store", n + 1, 2)]
            if b > 0 and more and (s, i) == (0, 6):
                o += [("qkv", n + 1, 0), ("store", n + 1, 0)]
            if b > 0 and more and (s, i) == (2, 2):
                o += [("qkv", n + 1, 1), ("store", n + 1, 1)]
            if b > 0 and (s, i) in ((1, 1), (1, 4)):
                o += [("wo", n - 1, i // 4)]
            if b + 2 < B:
                if (s, i) == (2, 6):
                    o += [("ln", n + 2)]
                if (s, i) in ((3, 1), (3, 4)):
                    o += [("xn", n + 2, i // 4)]
                if (s, i) == (3, 4):
                    o += [("store_xn", n + 2)]
            if not more:
                for at, x in {(2, 3): ("up", 0), (2, 5): ("up", 1), (2, 7): ("down", 0)}.items():
                    if at == (s, i):
                        o += [("split", L) + x]
                if (s, i) == (3, 4):
                    o += [("up", L, 0)]
    o += [("load_xf", L, 3), ("pv", u1 - 1, 1)]
    o += [("norm", u1 - 1, k) for k in range(4)]
    last = [("hidden", L, 0), ("wo", n0 + B - 1, 0), ("wo", n0 + B - 1, 1)]
    return o + ([("up", L, 1)] + last if L == 0 else last + [("up", L, 1)])


def ffn_order(L):
    C = CHUNKS[L]
    o = []
    start = attention_start(1) if L == 0 else []
    for c in range(2 * C + 1):
        if c < 2 * C:
            if c > 1:
                o += [("up", L, c)]
            if c > 0:
                o += [("hidden", L, c)]
            if c + 2 < 2 * C:
                o += [("split", L, "up", c + 2)]
        late = [x for x in start if x[0] == "load_q" and x[2] > 1]
        if L == 0 and c >= 2 * C - 8:
            fills = [x for x in start if x not in late]
            k = c - (2 * C - 8)
            share = -(-len(fills) // 8)
            o += fills[share * k:share * k + share // 2]
        if c + 1 < 2 * C:
            o += [("split", L, "down", c + 1)]
        if c >= 1:
            if (c - 1) % C == 0:
                o += [("bias", L, (c - 1) // C)]
            o += [("down", L, c - 1)]
            if (c - 1) % C == C - 1:
                h = (c - 1) // C
                o += [("add", L, h)]
                o += [("stats", 1, h)] if L == 0 else [("out", h)]
        if L == 0 and c >= 2 * C - 8:
            o += fills[share * k + share // 2:share * k + share]
        if L == 0 and c == 2 * C - 1:
            o += late
        if L == 0 and 2 * C - 14 <= c < 2 * C - 10:
            o += [("split", 1, "attn", c - (2 * C - 14))]
    return o


def program_order():
    o = [("stats", 0, 0)]
    start = attention_start(0)
    k = start.index(("qkv", 0, 2))
    o += start[:k] + [("split", 0, "attn", 0), ("split", 0, "attn", 1)] + start[k:]
    k = o.index(("qkv", 1, 0))
    o = o[:k] + [("split", 0, "attn", 2), ("split", 0, "attn", 3)] + o[k:]
    for L in range(2):
        o += attention_order(L) + ffn_order(L)
    return o


def work_banks(order, wk):
    bank, before, last = {}, {}, {}
    beside, turn = False, 0
    for x in order:
        if x[0] == "mt" and x[1] % (B * S) == B * S - 1:
            beside = True
        if x == ("st", B * S, 0):
            beside = False
        if x in wk:
            if beside:
                k = 3 if x[0] == "mt" and x[1] % (B * S) == B * S - 1 else (3, 7)[turn % 2]
            else:
                k = 3 + turn % 3
            turn += 1
            bank[x], before[x] = k, last.get(k)
            last[k] = x
    return bank, before


def numbered(order, *kinds):
    return {x: k for k, x in enumerate(x for x in order if x[0] in kinds)}


def build(nc, x_in, attn_w, up_w, down_w, up_b, qkv_b, out_b, rope, out):
    order = program_order()
    wk = numbered(order, "m", "mt", "xn", "qkv", "v", "wo")
    cp = numbered(order, "xn", "qkv")
    sp = numbered(order, "split")
    stg = numbered(order, "store")
    stt = numbered(order, "stats")
    lns = numbered(order, "ln")
    ups = numbered(order, "up")
    downs = numbered(order, "down")
    adds = numbered(order, "add")
    bank_of, before = work_banks(order, wk)
    units_done, hidden_done, count = {}, {}, {"pv": 0, "hidden": 0}
    for x in order:
        if x[0] == "hidden" or x[0] == "pv" and x[2] == 1:
            count[x[0]] += 1
        if x in wk:
            units_done[x], hidden_done[x] = count["pv"], count["hidden"]
    hips = {x: k for k, x in enumerate(x for x in order if x[0] == "qkv" and x[1] >= B)}

    qscr = nc.dram_tensor("q_parts", (2 * B, S, 2 * HD, UH * T), F32, kind="Internal").ap()
    kscr = nc.dram_tensor("k_parts", (2 * B, 4, HD, NKV * T), F32, kind="Internal").ap()
    xscr = nc.dram_tensor("xn_parts", (2, 2, P, 2 * KT, HALF), F32, kind="Internal").ap()

    with ExitStack() as ctx:
        def sb(name, shape, dt=F32):
            return ctx.enter_context(nc.sbuf_tensor(name, shape, dt))

        def sem(name):
            return ctx.enter_context(nc.semaphore(name))

        banks = ctx.enter_context(nc.psum_tensor("banks", [P, 8, 512], F32))
        x_res = sb("x_res", [P, NT, D])
        w_qkv = sb("w_qkv", [P, 2, KT, QKV], F32R)
        w_out = sb("w_out", [P, 2, S, D], F32R)
        raw = sb("raw", [P, 2, 1536])
        w_up = sb("w_up", [P, 2, 2, 1024], F32R)
        w_down = sb("w_down", [P, 2, 2, 512], F32R)
        xn = sb("xn", [P, TT, D])
        xnT = sb("xnT", [P, 2, KT, T], F32R)
        big = sb("big", [P, S, UH, T], F32R)
        k_max = sb("k_max", [ROWS, NKV, T], F32R)
        k_exp = sb("k_exp", [ROWS, NKV, T], F32R)
        v_t = sb("v_t", [P, T])
        v_sb = sb("v_sb", [P, TT, NKV, 2 * HD])
        stage = sb("stage", [P, 2, 2, 2, T], F32R)
        probs = sb("probs", [P, 8, 512])
        neg_max = sb("neg_max", [P, S, TT, UH])
        max_t = sb("max_t", [UH, 2, T], F32R)
        o_tok = sb("o_tok", [P, 2 * T])
        o_rec = sb("o_rec", [P, 16])
        o_div = sb("o_div", [P, T])
        o_t = sb("o_t", [P, T])
        ctxT = sb("ctxT", [P, 2, S, T], F32R)
        qkv_v = sb("qkv_v", [P, 2, T])
        rot_a = sb("rot_a", [P, 2, T])
        rot_b = sb("rot_b", [P, 2, T])
        table = sb("table", [P, 2, T])
        bias_qkv = sb("bias_qkv", [P, QKV // P])
        bias_up = sb("bias_up", [P, 24])
        bias_out = sb("bias_out", [P, 2, D], F32R)
        ones = sb("ones", [P, P], F32R)
        ident = sb("ident", [P, P])
        identb = sb("identb", [P, P], BF16)
        mask_qk = sb("mask_qk", [P, P], BF16)
        mask_kq = sb("mask_kq", [P, P], BF16)
        bn = sb("bn", [P, NT, 6])
        mv = sb("mv", [P, NT, 2])
        var_e = sb("var_e", [P, NT])
        dev = sb("dev", [P, NT])
        rs0 = sb("rs0", [P, NT])
        rs1 = sb("rs1", [P, NT])
        rstd = sb("rstd", [P, NT])

        hid = probs[:, :, :].rearrange("p (k s) t -> p k s t", k=4)
        hid_part = [[w_up[:, :, e, 512:1024] for e in range(2)],
                    [stage[:, :, e, :, :].rearrange("p k j t -> p k (j t)") for e in range(2)]]
        bias_raw = probs[:, 0:2, :]
        hid_f = hid[:, 0]
        gate_f = hid[:, 1]

        x_loaded = [sem(f"x_loaded{b}") for b in range(B)]
        c_loaded = sem("c_loaded")
        made = sem("made")
        identb_made = sem("identb_made")
        bias_split = sem("bias_split")
        raw_loaded = [sem(f"raw_loaded{k}") for k in range(2)]
        hi_split = sem("hi_split")
        lo_split = sem("lo_split")
        var_ready = sem("var_ready")
        dev_ready = sem("dev_ready")
        stat_steps = sem("stat_steps")
        ln_done = sem("ln_done")
        wk_filled = sem("wk_filled")
        wk_copied = sem("wk_copied")
        wk_emptied = sem("wk_emptied")
        xn_stored = sem("xn_stored")
        staged = [sem(f"staged{k}") for k in range(2)]
        q_loaded = [sem(f"q_loaded{k}") for k in range(S)]
        km_loaded = [sem(f"km_loaded{k}") for k in range(2)]
        ke_loaded = [sem(f"ke_loaded{k}") for k in range(2)]
        m_loaded = [sem(f"m_loaded{k}") for k in range(S)]
        st_filled = sem("st_filled")
        exp_done = sem("exp_done")
        pv_done = sem("pv_done")
        o_turned = sem("o_turned")
        o_inverted = sem("o_inverted")
        o_divided = sem("o_divided")
        o_back = sem("o_back")
        ctx_hi = sem("ctx_hi")
        ctx_lo = sem("ctx_lo")
        rot_cos = sem("rot_cos")
        rot_sin = sem("rot_sin")
        rot_done = sem("rot_done")
        rot_hi = sem("rot_hi")
        rot_lo = sem("rot_lo")
        xf_loaded = [sem(f"xf_loaded{k}") for k in range(2)]
        up_done = sem("up_done")
        hi_done = sem("hi_done")
        full_done = sem("full_done")
        gate_done = sem("gate_done")
        lo_done = sem("lo_done")
        bias_added = sem("bias_added")
        down_done = sem("down_done")
        added = sem("added")
        out_done = sem("out_done")

        def st_index(u, i):
            return 8 * u + i

        def unit(u):
            n, s = divmod(u, S)
            return n, s, s // 2

        def stores_in(layers, slot):
            return sum(k % 2 == slot for x, k in stg.items() if x[1] < B * layers)

        def work_bank(x):
            return bank_of[x]

        def last_fill(x, b):
            return [y for y in order[:order.index(x)] if bank_of.get(y) == b][-1]

        def stat_tiles(x):
            _, L, h = x
            w = TT if L == 0 else HT
            return range(w * h, w * h + w)

        def piece(L, what, k):
            if what == "attn":
                if k < 2:
                    return attn_w[L][:, k * 1536:(k + 1) * 1536], 1536, \
                        [w_qkv[:, h, 2 * k:2 * k + 2, :].rearrange("p k n -> p (k n)") for h in range(2)]
                at = KT * QKV + (k - 2) * 1024
                return attn_w[L][:, at:at + 1024], 1024, \
                    [w_out[:, h, 2 * (k - 2):2 * (k - 2) + 2, :].rearrange("p k n -> p (k n)") for h in range(2)]
            c = k % CHUNKS[L]
            if what == "up":
                n = 512 * (L + 1)
                return up_w[L][c], n, [w_up[:, k % 2, h, 0:n] for h in range(2)]
            return down_w[L][c], 512, [w_down[:, k % 2, h, :] for h in range(2)]

        def wait_weights_free(eng, L, what, k):
            if what == "attn" and L == 1:
                eng.wait_ge(wk_filled, wk[("wo", B - 1, 1)] + 1)
            if what == "up" and L == 1 and k < 2:
                eng.wait_ge(down_done, 2 * CHUNKS[0])
            if what == "up" and ups[("up", L, k)] >= 2:
                eng.wait_ge(up_done, ups[("up", L, k)] - 1)
            if what == "down" and downs[("down", L, k)] >= 2:
                eng.wait_ge(down_done, downs[("down", L, k)] - 1)

        IDENT, ZEROED, ONES_V, M_ROWS, ALL_MADE = 2, 3, 5, 6, 13

        block = ctx.enter_context(nc.Block())

        @block.sync
        def _(sp_):
            for b in range(B):
                sp_.dma_start(x_res[:, TT * b:TT * b + TT, :],
                              x_in[b].rearrange("(t p) d -> p t d", p=P)).then_inc(x_loaded[b], 16)
            for dst, src in ((table[:, :, :], rope), (bias_qkv[:, :], qkv_b), (bias_up[:, :], up_b)):
                sp_.dma_start(dst, src).then_inc(c_loaded, 16)
            sp_.wait_ge(made, ZEROED)
            for row in (0, 32):
                sp_.dma_start(bias_raw[row:row + 2, :, :], out_b).then_inc(c_loaded, 16)
            for x in order:
                if x[0] == "store_xn":
                    n = x[1]
                    L, b = divmod(n, B)
                    sp_.wait_ge(wk_emptied, wk[("xn", n, 1)] + 1)
                    if n >= 1:
                        sp_.wait_ge(xn_stored, 16 * n)
                    sp_.dma_start(xscr[L, b // 2, :, :, (b % 2) * T:(b % 2) * T + T],
                                  xnT[:, :, :, :].rearrange("p h k t -> p (h k) t").bitcast(F32)).then_inc(xn_stored, 16)
                if x[0] == "store":
                    _, n, pair = x
                    k = stg[x]
                    if n < B:
                        sp_.wait_ge(wk_emptied, wk[("qkv", n, pair)] + 1)
                    else:
                        sp_.wait_ge(rot_lo, hips[("qkv", n, pair)] + 1)
                    if pair < 2:
                        for j in range(2):
                            dst = qscr[n, 2 * pair + j].rearrange("(h d) (g t) -> (d g) h t", h=2, g=UH)
                            sp_.dma_start(dst, stage[:, k % 2, :, j, :].bitcast(F32)).then_inc(staged[k % 2], 16)
                    else:
                        for j in range(2):
                            dst = kscr[n].rearrange("(h e) d (g t) -> e (d g) h t", e=2, g=NKV)[j]
                            sp_.dma_start(dst, stage[:, k % 2, :, 0, :].bitcast(F32)).then_inc(staged[k % 2], 16)
                if x[0] == "load_q":
                    _, n, s = x
                    k = stg[("store", n, s // 2)]
                    sp_.wait_ge(staged[k % 2], 32 * (k // 2 + 1))
                    if n % B:
                        sp_.wait_ge(st_filled, st_index(S * (n - 1) + s, 7) + 1)
                    elif n:
                        sp_.wait_ge(up_done, ups[("up", 0, (s // 2 + 1) * CHUNKS[0] - 1)] + 1)
                    for e in range(2):
                        sp_.dma_start(big[32 * e:32 * e + 32, s, :, :].rearrange("p g t -> p (g t)").bitcast(F32),
                                      qscr[n, s]).then_inc(q_loaded[s], 16)
                if x[0] in ("load_km", "load_ke"):
                    kind, n, f = x
                    k = stg[("store", n, 2)]
                    sp_.wait_ge(staged[k % 2], 32 * (k // 2 + 1))
                    g = slice(4 * f * T, (4 * f + 4) * T)
                    buf, done = (k_max, km_loaded[f]) if kind == "load_km" else (k_exp, ke_loaded[f])
                    if n and kind == "load_km":
                        sp_.wait_ge(wk_filled, wk[("m", S * (n - 1) + 2 * f + 1, 7)] + 1)
                    elif n:
                        sp_.wait_ge(st_filled, st_index(S * (n - 1) + 2 * f + 1, 7) + 1)
                    sp_.dma_start(buf[0:4 * HD, 4 * f:4 * f + 4, :].rearrange("p g t -> p (g t)").bitcast(F32),
                                  kscr[n].rearrange("q d x -> (q d) x")[:, g]).then_inc(done, 16)
                if x[0] == "mrow":
                    u = x[1]
                    n, s, f = unit(u)
                    sp_.wait_ge(wk_emptied, wk[("mt", u)] + 1)
                    sp_.dma_start(big[MROW:MROW + 1, s, :, :].bitcast(F32),
                                  max_t[:, u % 2, :].bitcast(F32)).then_inc(m_loaded[s], 16)
                if x[0] == "load_xf":
                    _, L, e = x
                    h, part = divmod(e, 2)
                    sp_.wait_ge(xn_stored, 16 * B * (L + 1))
                    sp_.wait_ge(st_filled, st_index(S * (B * L + B - 1) + e, 7) + 1)
                    for rows in (slice(0, 64), slice(64, P)):
                        sp_.dma_start(big[rows, e, :, :].rearrange("p g t -> p (g t)").bitcast(F32),
                                      xscr[L, h, rows, part * KT:part * KT + KT].rearrange("p k t -> p (k t)")
                                      ).then_inc(xf_loaded[h], 16)
                if x[0] == "out":
                    h = x[1]
                    for t in range(HT):
                        tile = HT * h + t
                        sp_.wait_ge(added, 4 * adds[("add", 1, h)] + t + 1)
                        sp_.dma_start(out[tile // TT, (tile % TT) * P:(tile % TT) * P + P, :],
                                      x_res[:, tile, :]).then_inc(out_done, 16)
            sp_.wait_ge(out_done, 16 * NT)

        @block.gpsimd
        def _(pool):
            def load(k, x):
                src, n, _ = piece(*x[1:])
                pool.dma_start(raw[:, k % 2, 0:n], src).then_inc(raw_loaded[k % 2], 16)

            pieces = [x for x in order if x[0] == "split"]
            load(0, pieces[0])
            load(1, pieces[1])
            nc.gpsimd.memset(ident[:, :], 0.0).then_inc(made, 1)
            pool.wait_ge(made, 1)
            nc.gpsimd.affine_select(out=ident[:, :], in_=ident[:, :], compare_op=ALU.not_equal, fill=1.0,
                                    base=0, pattern=[[-1, P]], channel_multiplier=1).then_inc(made, 1)
            pool.wait_ge(made, IDENT)
            nc.gpsimd.memset(bias_raw[:, :, :], 0.0).then_inc(made, 1)
            pool.wait_ge(made, ZEROED)
            nc.gpsimd.memset(k_max[64:ROWS, :, :].bitcast(F32), 0.0).then_inc(made, 1)
            pool.wait_ge(made, 4)
            nc.gpsimd.memset(v_sb[:, :, :, :], 1.0).then_inc(made, 1)
            pool.wait_ge(made, ONES_V)
            nc.gpsimd.memset(big[64:ROWS, :, :, :].bitcast(F32), 0.0).then_inc(made, 1)
            pool.wait_ge(made, M_ROWS)
            nc.gpsimd.memset(k_exp[64:ROWS, :, :].bitcast(F32), 0.0).then_inc(made, 1)
            pool.wait_ge(made, 7)
            nc.gpsimd.memset(k_exp[MROW:MROW + 1, :, :].bitcast(F32), 1.0).then_inc(made, 1)
            pool.wait_ge(made, 8)
            nc.gpsimd.memset(ones[:, :].bitcast(F32), 1.0).then_inc(made, 1)
            pool.wait_ge(made, 9)
            nc.gpsimd.memset(mask_qk[:, :], 0.0).then_inc(made, 1)
            pool.wait_ge(made, 10)
            nc.gpsimd.memset(mask_kq[:, :], 0.0).then_inc(made, 1)
            pool.wait_ge(made, 11)
            nc.gpsimd.affine_select(out=mask_qk[:, :], in_=mask_qk[:, :], compare_op=ALU.is_ge, fill=MASKED,
                                    base=0, pattern=[[-1, P]], channel_multiplier=1).then_inc(made, 1)
            pool.wait_ge(made, 12)
            nc.gpsimd.affine_select(out=mask_kq[:, :], in_=mask_kq[:, :], compare_op=ALU.is_ge, fill=MASKED,
                                    base=0, pattern=[[1, P]], channel_multiplier=-1).then_inc(made, 1)
            pool.wait_ge(made, ALL_MADE)
            last = [(made, ALL_MADE)]

            def in_order():
                pool.wait_ge(*last[0])

            for x in order:
                if x[0] == "split" and sp[x] + 2 < len(pieces):
                    pool.wait_ge(lo_split, sp[x] + 1)
                    load(sp[x] + 2, pieces[sp[x] + 2])
                if x[0] == "norm" and x[2] == 3:
                    u = x[1]
                    n, s, f = unit(u)
                    pool.wait_ge(ctx_hi, u + 1)
                    in_order()
                    nc.gpsimd.tensor_tensor(ctxT[:, 1, s, :], o_t[:, :], ctxT[:, 0, s, :].bitcast(F32),
                                            ALU.subtract).then_inc(ctx_lo, 1)
                    last[0] = (ctx_lo, u + 1)
                if x[0] == "qkv" and x[1] >= B:
                    _, n, pair = x
                    w = 2 if pair < 2 else 1
                    k = stg[("store", n, pair)]
                    pool.wait_ge(wk_copied, cp[x] + 1)
                    if hips[x]:
                        pool.wait_ge(rot_done, hips[x])
                    in_order()
                    nc.gpsimd.tensor_tensor(rot_a[:, 0:w, :], qkv_v[:, 0:w, :],
                                            table[:, 0:1, :].to_broadcast([P, w, T]), ALU.mult).then_inc(rot_cos, 1)
                    last[0] = (rot_cos, hips[x] + 1)
                    pool.wait_ge(rot_hi, hips[x] + 1)
                    in_order()
                    nc.gpsimd.tensor_tensor(stage[:, k % 2, 1, 0:w, :], rot_b[:, 0:w, :],
                                            stage[:, k % 2, 0, 0:w, :].bitcast(F32), ALU.subtract).then_inc(rot_lo, 1)
                    last[0] = (rot_lo, hips[x] + 1)

        @block.tensor
        def _(pe):
            def work(x):
                k, y = bank_of[x], before[x]
                if y:
                    pe.wait_ge(wk_emptied, wk[y] + 1)
                if k == 7 and (not y or units_done[x] > units_done[y]):
                    pe.wait_ge(o_turned, units_done[x])
                if k in (4, 5) and y and hidden_done[x] > hidden_done[y]:
                    pe.wait_ge(lo_done, hidden_done[x])
                return k

            def three(out_ap, lhs, rhs, first, last, **kw):
                for j, (a, b_) in enumerate(((0, 0), (1, 0), (0, 1))):
                    mm = nc.tensor.matmul(out_ap, lhs(a), rhs(b_), start=first and j == 0, stop=last and j == 2, **kw)
                return mm

            pe.wait_ge(made, IDENT)
            for x in order:
                if x[0] == "xn":
                    _, n, t = x
                    k = work(x)
                    pe.wait_ge(ln_done, TT * n + t + 1)
                    for c in range(KT):
                        mm = nc.tensor.transpose(banks[:, k, c * P:c * P + P], xn[:, t, c * P:c * P + P], ident[:, :])
                    mm.then_inc(wk_filled, 1)
                if x[0] == "qkv":
                    _, n, pair = x
                    k = work(x)
                    pe.wait_ge(wk_emptied, wk[("xn", n, 1)] + 1)
                    pe.wait_ge(lo_split, sp[("split", n // B, "attn", 1)] + 1)
                    for j in range(2):
                        m = (2 * pair + j) * P
                        for c in range(KT):
                            mm = three(banks[:, k, j * T:j * T + T],
                                       lambda h: w_qkv[:, h, c, m:m + P], lambda h: xnT[:, h, c, :],
                                       c == 0, c == KT - 1)
                    mm.then_inc(wk_filled, 1)
                if x[0] == "v":
                    n = x[1]
                    k = work(x)
                    pe.wait_ge(wk_copied, cp[("qkv", n, 2)] + 1)
                    for t in range(TT):
                        mm = nc.tensor.transpose(banks[:, k, t * P:t * P + P], v_t[:, t * P:t * P + P], ident[:, :])
                    mm.then_inc(wk_filled, 1)
                if x[0] == "m":
                    _, u, i = x
                    n, s, f = unit(u)
                    t, g = divmod(i, 4)
                    k = work(x)
                    if x == ("m", 0, 0):
                        pe.wait_ge(made, M_ROWS)
                    if x == ("m", B * S, 0):
                        pe.wait_ge(identb_made, 1)
                    if i == 0:
                        pe.wait_ge(q_loaded[s], 32 * (n + 1))
                        pe.wait_ge(km_loaded[f], 16 * (n + 1))
                    for r in range(2):
                        mm = nc.tensor.matmul(banks[:, k, r * T:r * T + T],
                                              big[0:ROWS, s, 2 * g + r, t * P:t * P + P], k_max[0:ROWS, 4 * f + g, :],
                                              start=r == 0, stop=n < B and r == 1, skip_group_check=True)
                    if n >= B:
                        diagonal = banks[:, k, :].rearrange("p (r t) -> p r t", r=2)[:, :, t * P:t * P + P]
                        mm = nc.tensor.matmul(diagonal, identb[:, :], mask_qk[:, None, :].to_broadcast([P, 2, P]),
                                              start=False, stop=True, skip_group_check=True)
                    mm.then_inc(wk_filled, 1)
                if x[0] == "mt":
                    u = x[1]
                    n, s, f = unit(u)
                    k = work(x)
                    pe.wait_ge(wk_emptied, wk[("m", u, 7)] + 1)
                    for t in range(TT):
                        mm = nc.tensor.transpose(banks[0:UH, k, t * P:t * P + P], neg_max[:, s, t, :], ident[:, :])
                    mm.then_inc(wk_filled, 1)
                if x[0] == "st":
                    _, u, i = x
                    n, s, f = unit(u)
                    t, g = divmod(i, 4)
                    k = st_index(u, i)
                    if k >= 3:
                        pe.wait_ge(exp_done, k - 2)
                    if k == 0:
                        pe.wait_ge(made, ALL_MADE)
                    if x == ("st", B * S, 0):
                        pe.wait_ge(added, NT)
                    if i == 0:
                        pe.wait_ge(m_loaded[s], 16 * (n + 1))
                        pe.wait_ge(ke_loaded[f], 16 * (n + 1))
                    keys = k_exp[0:ROWS, 4 * f + g, t * P:t * P + P]
                    bank = banks[:, k % 3, :].rearrange("p (r t) -> p r t", r=2)
                    if n < B:
                        mm = nc.tensor.matmul(bank, keys, big[0:ROWS, s, 2 * g:2 * g + 2, :], start=True, stop=True)
                    else:
                        q0 = t * P
                        part = bank if t == 0 else banks[:, k % 3, 0:2 * P].rearrange("p (r t) -> p r t", r=2)
                        nc.tensor.matmul(part, keys, big[0:ROWS, s, 2 * g:2 * g + 2, q0:], start=True, stop=False,
                                         skip_group_check=True)
                        mm = nc.tensor.matmul(part[:, :, 0:P], identb[:, :], mask_kq[:, None, :].to_broadcast([P, 2, P]),
                                              start=False, stop=True, skip_group_check=True)
                    mm.then_inc(st_filled, 1)
                if x[0] == "pv":
                    _, u, t = x
                    n, s, f = unit(u)
                    pe.wait_ge(exp_done, st_index(u, 4 * t + 3) + 1)
                    if t == 0 and u >= 2:
                        pe.wait_ge(o_turned, u - 1)
                    if x == ("pv", B * S, 0):
                        pe.wait_ge(added, NT)
                    if x == ("pv", B * S + 1, 0):
                        pe.wait_ge(wk_emptied, wk[last_fill(x, 7)] + 1)
                    if t == 0 and s == 0:
                        pe.wait_ge(wk_emptied, wk[("v", n)] + 1)
                    for g in range(4):
                        o = banks[32 * g:32 * g + 32, 6 + u % 2, :]
                        p_ = probs[:, 4 * t + g, :]
                        if n >= B and t == 1:
                            o = o.rearrange("p (r t) -> p r t", r=2)[:, :, P:2 * P]
                            p_ = p_[:, 0:2 * P].rearrange("p (r t) -> p r t", r=2)
                        mm = nc.tensor.matmul(o, v_sb[:, t, 4 * f + g, :], p_, start=t == 0, stop=t == 1,
                                              skip_group_check=True)
                    mm.then_inc(pv_done, 1)
                if x[0] == "wo":
                    _, n, t = x
                    k = work(x)
                    pe.wait_ge(ctx_lo, S * (n + 1))
                    pe.wait_ge(lo_split, sp[("split", n // B, "attn", 3)] + 1)
                    for s in range(S):
                        mm = three(banks[:, k, :], lambda h: ctxT[:, h, s, t * P:t * P + P],
                                   lambda h: w_out[:, h, s, :], s == 0, s == S - 1)
                    mm.then_inc(wk_filled, 1)
                if x[0] == "up":
                    _, L, c = x
                    h = c // CHUNKS[L]
                    pe.wait_ge(lo_split, sp[("split", L, "up", c)] + 1)
                    if c % CHUNKS[L] == 0:
                        pe.wait_ge(xf_loaded[h], 64 * (L + 1))
                    hid_banks = [HID[c % 2]] if L == 0 else [HID[2 * (c % 2)], HID[2 * (c % 2) + 1]]
                    if c < 2:
                        for k in hid_banks:
                            pe.wait_ge(wk_emptied, wk[last_fill(x, k)] + 1)
                        if 7 in hid_banks:
                            pe.wait_ge(o_turned, B * S * (L + 1))
                    else:
                        pe.wait_ge(lo_done, ups[x] - 1)
                    xf = big[:, 2 * h:2 * h + 2, :, :].rearrange("p a g t -> p (a g t)").rearrange(
                        "p (h k t) -> p h k t", h=2, k=KT)
                    for j, k in enumerate(hid_banks):
                        for q in range(KT):
                            mm = three(banks[:, k, :],
                                       lambda e: w_up[:, c % 2, e, (j * KT + q) * P:(j * KT + q) * P + P],
                                       lambda e: xf[:, e, q, :], q == 0, q == KT - 1)
                    mm.then_inc(up_done, 1)
                if x[0] == "bias":
                    _, L, h = x
                    if h == 0:
                        pe.wait_ge(exp_done, 8 * B * S * (L + 1))
                        pe.wait_ge(o_turned, B * S * (L + 1))
                    else:
                        pe.wait_ge(added, 4 * (2 * L + h))
                    pe.wait_ge(bias_split, 1)
                    for t in range(HT):
                        nc.tensor.matmul(banks[:, ACC[t], :], ones[:, :], bias_out[:, L, :],
                                         start=True, stop=False, skip_group_check=True)
                if x[0] == "down":
                    _, L, c = x
                    pe.wait_ge(lo_split, sp[("split", L, "down", c)] + 1)
                    pe.wait_ge(lo_done, downs[x] + 1)
                    for t in range(HT):
                        mm = three(banks[:, ACC[t], :], lambda h: hid_part[L][h][:, c % 2, t * P:t * P + P],
                                   lambda h: w_down[:, c % 2, h, :], False, c % CHUNKS[L] == CHUNKS[L] - 1,
                                   skip_group_check=True)
                    mm.then_inc(down_done, 1)

        @block.scalar
        def _(act):
            copies = 0
            for x in order:
                if x[0] == "split":
                    k = sp[x]
                    _, n, parts = piece(*x[1:])
                    act.wait_ge(raw_loaded[k % 2], 16 * (k // 2 + 1))
                    wait_weights_free(act, *x[1:])
                    nc.scalar.copy(parts[0], raw[:, k % 2, 0:n]).then_inc(hi_split, 1)
                if x[0] == "stats":
                    k = stt[x]
                    tiles = stat_tiles(x)
                    t = slice(tiles[0], tiles[-1] + 1)
                    act.wait_ge(var_ready, k + 1)
                    nc.scalar.activation(dev[:, t], var_e[:, t], ACT.Sqrt).then_inc(dev_ready, 1)
                if x[0] == "xn":
                    _, n, t = x
                    act.wait_ge(wk_filled, wk[x] + 1)
                    if n and t == 0:
                        act.wait_ge(wk_filled, max(wk[("qkv", n - 1, j)] for j in range(3)) + 1)
                        act.wait_ge(xn_stored, 16 * n)
                    nc.scalar.copy(xnT[:, 0, :, t * P:t * P + P],
                                   banks[:, work_bank(x), :].rearrange("p (k t) -> p k t", k=KT)).then_inc(wk_copied, 1)
                if x[0] == "qkv":
                    _, n, pair = x
                    k = stg[("store", n, pair)]
                    w = 2 if pair < 2 else 1
                    bank = banks[:, work_bank(x), :].rearrange("p (j t) -> p j t", j=2)
                    act.wait_ge(wk_filled, wk[x] + 1)
                    if n < B:
                        if k >= 2:
                            act.wait_ge(staged[k % 2], 32 * (k // 2))
                        ins = nc.scalar.copy(stage[:, k % 2, 0, 0:w, :], bank[:, 0:w, :])
                    else:
                        if hips[x]:
                            act.wait_ge(rot_cos, hips[x])
                            act.wait_ge(wk_emptied, wk[next(y for y, k_ in hips.items() if k_ == hips[x] - 1)] + 1)
                        for j in range(w):
                            ins = nc.scalar.activation(qkv_v[:, j, :], bank[:, j, :], ACT.Identity,
                                                       bias=bias_qkv[:, 2 * pair + j:2 * pair + j + 1])
                    if pair == 2:
                        if n % B:
                            act.wait_ge(wk_filled, wk[("v", n - 1)] + 1)
                        elif n:
                            act.wait_ge(wk_filled, wk[("v", n - 1)] + 1)
                        if n < B:
                            ins = nc.scalar.copy(v_t[:, :], bank[:, 1, :])
                        else:
                            ins = nc.scalar.activation(v_t[:, :], bank[:, 1, :], ACT.Identity, bias=bias_qkv[:, 5:6])
                    ins.then_inc(wk_copied, 1)
                    if n >= B:
                        act.wait_ge(rot_done, hips[x] + 1)
                        act.wait_ge(staged[k % 2], 32 * (k // 2))
                        nc.scalar.copy(stage[:, k % 2, 0, 0:w, :], rot_b[:, 0:w, :]).then_inc(rot_hi, 1)
                if x[0] == "st":
                    _, u, i = x
                    n, s, f = unit(u)
                    t = i // 4
                    k = st_index(u, i)
                    act.wait_ge(st_filled, k + 1)
                    if k == 0:
                        act.wait_ge(bias_split, 1)
                    if x == ("st", B * S, 0):
                        act.wait_ge(lo_done, 2 * CHUNKS[0])
                    if u:
                        act.wait_ge(pv_done, 2 * (u - 1) + t + 1)
                    w = 2 * P if n >= B and t == 1 else 512
                    nc.scalar.activation(probs[:, i, 0:w], banks[:, k % 3, 0:w], ACT.Exp,
                                         scale=SCALES[n // B]).then_inc(exp_done, 1)
                if x[0] == "norm" and x[2] == 3:
                    u = x[1]
                    n, s, f = unit(u)
                    act.wait_ge(o_back, u + 1)
                    if n and s == 0:
                        act.wait_ge(wk_filled, wk[("wo", n - 1, 1)] + 1)
                    nc.scalar.copy(ctxT[:, 0, s, :], o_t[:, :]).then_inc(ctx_hi, 1)
                if x[0] == "hidden":
                    _, L, c = x
                    k = ups[("up", L, c)]
                    hid_hi = hid_part[L][0]
                    act.wait_ge(up_done, k + 1)
                    act.wait_ge(c_loaded, 80)
                    cc = c % CHUNKS[L]
                    if c == 0:
                        act.wait_ge(pv_done, 2 * B * S * (L + 1) - 1)
                    if c == 0 and L == 1:
                        for e in range(2):
                            act.wait_ge(staged[e], 32 * stores_in(L + 1, e))
                    if L == 0:
                        bias = bias_up[:, cc:cc + 1]
                        if k >= 2:
                            act.wait_ge(down_done, k - 1)
                            act.wait_ge(lo_done, k - 1)
                        nc.scalar.activation(hid_hi[:, c % 2, :], banks[:, HID[c % 2], :], ACT.Gelu_apprx_tanh,
                                             bias=bias).then_inc(hi_done, 1)
                        nc.scalar.activation(hid_f[:, c % 2, :], banks[:, HID[c % 2], :], ACT.Gelu_apprx_tanh,
                                             bias=bias).then_inc(full_done, 1)
                    else:
                        act.wait_ge(lo_done, k - 1)
                        nc.scalar.activation(gate_f[:, c % 2, :], banks[:, HID[2 * (c % 2)], :], ACT.Silu,
                                             bias=bias_up[:, 16 + cc:17 + cc]).then_inc(gate_done, 1)
                        act.wait_ge(full_done, k + 1)
                        act.wait_ge(down_done, k - 1)
                        nc.scalar.copy(hid_hi[:, c % 2, :], hid_f[:, c % 2, :]).then_inc(hi_done, 1)

        @block.vector
        def _(dve):
            steps = [0]

            def link(ins):
                steps[0] += 1
                ins.then_inc(stat_steps, 1)
                dve.wait_ge(stat_steps, steps[0])

            for x in order:
                if x[0] == "split":
                    k = sp[x]
                    _, n, parts = piece(*x[1:])
                    dve.wait_ge(hi_split, k + 1)
                    nc.vector.tensor_tensor(parts[1], raw[:, k % 2, 0:n], parts[0].bitcast(F32),
                                            ALU.subtract).then_inc(lo_split, 1)
                if x[0] == "stats":
                    _, L, h = x
                    k = stt[x]
                    tiles = stat_tiles(x)
                    for t in tiles:
                        if L == 0:
                            dve.wait_ge(x_loaded[t // TT], 16)
                        else:
                            dve.wait_ge(added, t + 1)
                        ins = nc.vector.bn_stats(bn[:, t, :], x_res[:, t, :])
                        link(ins)
                        ins = nc.vector.bn_aggr(mv[:, t, :], bn[:, t, :])
                    link(ins)
                    t = slice(tiles[0], tiles[-1] + 1)
                    nc.vector.tensor_scalar(var_e[:, t], mv[:, t, 1], EPS, None, ALU.add).then_inc(var_ready, 1)
                    dve.wait_ge(dev_ready, k + 1)
                    link(nc.vector.reciprocal(rs0[:, t], dev[:, t]))
                    link(nc.vector.tensor_tensor(rs1[:, t], rs0[:, t], rs0[:, t], ALU.mult))
                    link(nc.vector.tensor_tensor(rs1[:, t], rs1[:, t], var_e[:, t], ALU.mult))
                    link(nc.vector.tensor_scalar(rs1[:, t], rs1[:, t], -0.5, 1.5, ALU.mult, ALU.add))
                    link(nc.vector.tensor_tensor(rstd[:, t], rs0[:, t], rs1[:, t], ALU.mult))
                    if x == ("stats", 0, B - 1):
                        nc.vector.tensor_copy(identb[:, :], ident[:, :]).then_inc(identb_made, 1)
                        dve.wait_ge(c_loaded, 80)
                        link(nc.vector.tensor_copy(bias_out[:, :, :], bias_raw[:, :, :]))
                        nc.vector.tensor_tensor(bias_out[32:64, :, :], bias_raw[32:64, :, :],
                                                bias_out[32:64, :, :].bitcast(F32), ALU.subtract).then_inc(bias_split, 1)
                if x[0] == "ln":
                    n = x[1]
                    for t in range(TT):
                        tile = TT * (n % B) + t
                        if n:
                            dve.wait_ge(wk_filled, wk[("xn", n - 1, t)] + 1)
                        nc.vector.tensor_scalar(xn[:, t, :], x_res[:, tile, :], mv[:, tile, 0:1], rstd[:, tile:tile + 1],
                                                ALU.subtract, ALU.mult).then_inc(ln_done, 1)
                if x[0] == "xn":
                    _, n, t = x
                    dve.wait_ge(wk_copied, cp[x] + 1)
                    nc.vector.tensor_tensor(xnT[:, 1, :, t * P:t * P + P],
                                            banks[:, work_bank(x), :].rearrange("p (k t) -> p k t", k=KT),
                                            xnT[:, 0, :, t * P:t * P + P].bitcast(F32), ALU.subtract).then_inc(wk_emptied, 1)
                if x[0] == "qkv":
                    _, n, pair = x
                    k = stg[("store", n, pair)]
                    w = 2 if pair < 2 else 1
                    dve.wait_ge(wk_copied, cp[x] + 1)
                    if n < B:
                        bank = banks[:, work_bank(x), :].rearrange("p (j t) -> p j t", j=2)
                        nc.vector.tensor_tensor(stage[:, k % 2, 1, 0:w, :], bank[:, 0:w, :],
                                                stage[:, k % 2, 0, 0:w, :].bitcast(F32), ALU.subtract).then_inc(wk_emptied, 1)
                    else:
                        if hips[x]:
                            dve.wait_ge(rot_lo, hips[x])
                        other = table[:, 1:2, :]
                        nc.vector.tensor_tensor(rot_b[0:64, 0:w, :], qkv_v[64:P, 0:w, :],
                                                other[64:P].to_broadcast([64, w, T]), ALU.mult).then_inc(rot_sin, 1)
                        nc.vector.tensor_tensor(rot_b[64:P, 0:w, :], qkv_v[0:64, 0:w, :],
                                                other[0:64].to_broadcast([64, w, T]), ALU.mult).then_inc(wk_emptied, 1)
                        dve.wait_ge(rot_sin, hips[x] + 1)
                        dve.wait_ge(wk_emptied, wk[x] + 1)
                        dve.wait_ge(rot_cos, hips[x] + 1)
                        nc.vector.tensor_tensor(rot_b[:, 0:w, :], rot_b[:, 0:w, :], rot_a[:, 0:w, :],
                                                ALU.add).then_inc(rot_done, 1)
                if x[0] == "v":
                    n = x[1]
                    dve.wait_ge(wk_filled, wk[x] + 1)
                    if n == 0:
                        dve.wait_ge(made, ONES_V)
                    if n:
                        dve.wait_ge(pv_done, 2 * S * n)
                    nc.vector.tensor_copy(v_sb[:, :, :, 0:HD],
                                          banks[:, work_bank(x), 0:TT * P].rearrange("p (t g d) -> p t g d", t=TT, g=NKV)
                                          ).then_inc(wk_emptied, 1)
                if x[0] == "m":
                    _, u, i = x
                    n, s, f = unit(u)
                    t, g = divmod(i, 4)
                    dve.wait_ge(wk_filled, wk[x] + 1)
                    if n:
                        dve.wait_ge(wk_filled, wk[("mt", u - S)] + 1)
                    w = T if n < B or t == 1 else P
                    nc.vector.tensor_reduce(neg_max[:, s, t, 2 * g:2 * g + 2],
                                            banks[:, work_bank(x), :].rearrange("p (r t) -> p r t", r=2)[:, :, 0:w],
                                            AX.X, ALU.max, negate=True).then_inc(wk_emptied, 1)
                if x[0] == "mt":
                    u = x[1]
                    n, s, f = unit(u)
                    dve.wait_ge(wk_filled, wk[x] + 1)
                    if u >= 2:
                        dve.wait_ge(m_loaded[(u - 2) % S], 16 * ((u - 2) // S + 1))
                    nc.vector.tensor_copy(max_t[:, u % 2, :], banks[0:UH, work_bank(x), 0:T]).then_inc(wk_emptied, 1)
                if x[0] == "norm":
                    _, u, k = x
                    if k == 0:
                        dve.wait_ge(pv_done, 2 * u + 2)
                        if u:
                            dve.wait_ge(o_divided, u)
                        nc.vector.transpose(o_tok[:, :], banks[:, 6 + u % 2, :]).then_inc(o_turned, 1)
                    by = o_tok[:, :].rearrange("p (r q c) -> p r q c", r=2, q=8)
                    if k == 1:
                        dve.wait_ge(o_turned, u + 1)
                        nc.vector.reciprocal(o_rec[:, :].rearrange("p (r q) -> p r q", r=2), by[:, :, :, HD]).then_inc(o_inverted, 1)
                    if k == 2:
                        dve.wait_ge(o_inverted, u + 1)
                        if u:
                            dve.wait_ge(o_back, u)
                        nc.vector.tensor_tensor(o_div[:, :].rearrange("p (q r c) -> p r q c", r=2, c=HD), by[:, :, :, 0:HD],
                                                o_rec[:, :].rearrange("p (r q a) -> p r q a", r=2, a=1).to_broadcast([P, 2, 8, HD]),
                                                ALU.mult).then_inc(o_divided, 1)
                    if k == 3:
                        dve.wait_ge(o_divided, u + 1)
                        if u:
                            dve.wait_ge(ctx_lo, u)
                        nc.vector.transpose(o_t[:, :], o_div[:, :]).then_inc(o_back, 1)
                if x[0] == "wo":
                    _, n, t = x
                    tile = TT * (n % B) + t
                    dve.wait_ge(wk_filled, wk[x] + 1)
                    nc.vector.tensor_tensor(x_res[:, tile, :], x_res[:, tile, :], banks[:, work_bank(x), :],
                                            ALU.add).then_inc(wk_emptied, 1)
                if x[0] == "hidden":
                    _, L, c = x
                    k = ups[("up", L, c)]
                    hid_hi, hid_lo = hid_part[L]
                    cc = c % CHUNKS[L]
                    if L == 1:
                        dve.wait_ge(gate_done, k - 2 * CHUNKS[0] + 1)
                        nc.vector.scalar_tensor_tensor(out=hid_f[:, c % 2, :], in0=banks[:, HID[2 * (c % 2) + 1], :],
                                                       scalar=bias_up[:, 20 + cc:21 + cc], in1=gate_f[:, c % 2, :],
                                                       op0=ALU.add, op1=ALU.mult).then_inc(full_done, 1)
                    dve.wait_ge(hi_done, k + 1)
                    dve.wait_ge(full_done, k + 1)
                    if k >= 2:
                        dve.wait_ge(down_done, k - 1)
                    nc.vector.tensor_tensor(hid_lo[:, c % 2, :], hid_f[:, c % 2, :], hid_hi[:, c % 2, :].bitcast(F32),
                                            ALU.subtract).then_inc(lo_done, 1)
                if x[0] == "add":
                    _, L, h = x
                    dve.wait_ge(down_done, downs[("down", L, (h + 1) * CHUNKS[L] - 1)] + 1)
                    for t in range(HT):
                        nc.vector.tensor_tensor(x_res[:, HT * h + t, :], x_res[:, HT * h + t, :], banks[:, ACC[t], :],
                                                ALU.add).then_inc(added, 1)


_PERM_HEAD = [[4 * (4 * (s // 2) + g) + 2 * (s % 2) + r for g in range(4) for r in range(2)] for s in range(S)]


def _layouts(i):
    def q_rows(head_row):
        return np.array([head_row(_PERM_HEAD[s][h]) + d for s in range(S) for d in range(HD) for h in range(UH)])

    def kd(base):
        return np.array([base(g) + d for d in range(HD) for g in range(NKV)])

    def gd(base):
        return np.array([base(g) + d for g in range(NKV) for d in range(HD)])

    def by_part(w):
        return w.T.reshape(KT, P, -1).transpose(1, 0, 2)

    block = (REP + 2) * HD
    w0 = np.concatenate([i["L0_attn_Wq"][q_rows(lambda h: h * HD)], i["L0_attn_Wk"][kd(lambda g: g * HD)],
                         i["L0_attn_Wv"][gd(lambda g: g * HD)]])
    rows1 = np.concatenate([q_rows(lambda h: (h // REP) * block + (h % REP) * HD),
                            kd(lambda g: g * block + REP * HD), gd(lambda g: g * block + (REP + 1) * HD)])
    w1 = i["L1_attn_w_qkv"][rows1]
    cols = np.array([_PERM_HEAD[s][h] * HD + d for s in range(S) for h in range(UH) for d in range(HD)])
    outs = [by_part(w[:, cols]) for w in (i["L0_attn_Wo"], i["L1_attn_w_dense"])]
    attn = [np.concatenate([by_part(w).reshape(P, -1), o.reshape(P, -1)], 1) for w, o in zip((w0, w1), outs)]
    up0 = i["L0_ffn_W1"].reshape(KT, P, CHUNKS[0], P).transpose(2, 1, 0, 3).reshape(CHUNKS[0], P, -1)
    up1 = i["L1_ffn_w12"].reshape(2, CHUNKS[1], P, KT, P).transpose(1, 4, 0, 3, 2).reshape(CHUNKS[1], P, -1)
    down0 = i["L0_ffn_W2"].reshape(CHUNKS[0], P, D)
    down1 = i["L1_ffn_w3"].T.reshape(CHUNKS[1], P, D)
    up_b = np.concatenate([i["L0_ffn_fc1_bias"].reshape(-1, P), i["L1_ffn_b12"].reshape(-1, P)]).T
    zero = np.zeros(D, np.float32)
    out_b = np.stack([np.stack([i["L0_ffn_fc2_bias"], i["L1_ffn_b3"]]), np.stack([zero, i["L1_attn_b_dense"]])])
    inv = (np.float32(1.0) / np.power(np.float32(1e6), np.arange(0, HD, 2, dtype=np.float32) / np.float32(HD))).astype(np.float32)
    ang = np.outer(inv, np.arange(T, dtype=np.float32)).astype(np.float32)
    cos, sin = np.cos(ang), np.sin(ang)
    row = np.arange(P) // 8
    rope = np.stack([cos[row % 8], np.where((row < 8)[:, None], sin[row % 8], -sin[row % 8])], 1).astype(np.float32)
    c = np.ascontiguousarray
    return {"x": c(i["L0_attn_x"]), "attn0": c(attn[0]), "attn1": c(attn[1]), "up0": c(up0), "up1": c(up1),
            "down0": c(down0), "down1": c(down1), "up_b": c(up_b), "qkv_b": c(i["L1_attn_b_qkv"][rows1].reshape(-1, P).T),
            "out_b": c(out_b), "rope": c(rope)}


def kernel(**inputs):
    import concourse.bacc as _bacc
    from concourse.bass_utils import run_bass_kernel_spmd as _run

    nc = _bacc.Bacc("TRN2", target_bir_lowering=False, num_devices=1)
    arrays = _layouts({k: np.asarray(v) for k, v in inputs.items()})
    a = {k: nc.dram_tensor(f"in_{k}", v.shape, F32, kind="ExternalInput").ap() for k, v in arrays.items()}
    out = nc.dram_tensor("out", (B, T, D), F32, kind="ExternalOutput").ap()
    build(nc, a["x"], [a["attn0"], a["attn1"]], [a["up0"], a["up1"]], [a["down0"], a["down1"]],
          a["up_b"], a["qkv_b"], a["out_b"], a["rope"], out)
    r = _run(nc, [{f"in_{k}": v for k, v in arrays.items()}], core_ids=[0])
    return r.results[0]["out"]
```

```python
from contextlib import ExitStack

import numpy as np

import concourse.bass as bass
from concourse import mybir

F32 = mybir.dt.float32
F32R = mybir.dt.float32r
BF16 = mybir.dt.bfloat16
ALU = mybir.AluOpType
ACT = mybir.ActivationFunctionType
AX = mybir.AxisListType

P = 128
B, T, D = 4, 256, 512
HD = 16
NH, NKV = 32, 8
REP = NH // NKV
KT = D // P
QKV = (NH + 2 * NKV) * HD
S = 4
UH = NH // S
TT = T // P
NT = B * TT
HALF = B * T // 2
HT = HALF // P
ROWS = 96
MROW = 4 * HD
EPS = 1e-5
SCALES = (1.0 / 4.0, 1.0 / 16.0)
MASKED = -1e38
CHUNKS = (2048 // P, 512 // P)
ACC = (0, 1, 2, 6)
RAW = 3
BESIDE = 10
EARLY = 5
AT = {"pv1": (2, 3), "mt": (2, 2), "norm": (4, 3), "pv0": (7, 6), "v": (2, 5), "keys": (4, 2),
      "queries": (13, 14), "wo0": (8, 9), "wo1": (11, 10), "ln": (19, 21), "xn": (23, 23),
      "weights": ((19, 21, 23), (19, 21, 23)), "hidden": ((25, 3), (25, 5))}
HID = (5, 4, 3, 7)


def parts(x):
    count = KT * (x[1] + 1) if x[0] == "up" else 4
    return [("part", x, p) for p in range(count - 1)] + [x]


def direct(x):
    return x[0] == "qkv" and (x[1] == 0 or x[1] == 1 and x[2] < 2)


def project(n, pair):
    x = ("qkv", n, pair)
    return parts(x) + [("drain", x)] + ([("round", x)] if n >= B else []) + [("store", n, pair)]


def transposed(n):
    return [x for t in range(TT) for x in (("xn", n, t), ("drain", ("xn", n, t)))] + [("store_xn", n)]


def woven(main, side, early=0):
    o, done = [], 0
    for k, x in enumerate(main):
        o.append(x)
        want = min(len(side) * (k + 1) // (len(main) - early), len(side))
        o += side[done:want]
        done = want
    return o


def attention_start(L):
    n0, u0 = B * L, B * S * L
    first = L == 0
    o = [("ln", n0)] + [("split", L, "attn", 2)] * first + transposed(n0)
    if first:
        o += [("split", L, "attn", 0), ("stats", L, 1), ("root", L, 1), ("rstd", L, 1)]
    o += [("ln", n0 + 1)]
    for pair in (2, 0):
        o += project(n0, pair) + [("split", L, "attn", 1)] * (first and pair == 2)
    o += [("load_km", n0, 0), ("load_q", n0, 0)] + [("load_q", n0, 1)]
    o += project(n0, 1) + [("load_ke", n0, 0)]
    o += transposed(n0 + 1) + [("v", n0)]
    for pair, u in ((0, u0), (1, u0 + 1)):
        proj = project(n0 + 1, pair)
        ms = [("m", u, i) for i in range(8)]
        o += woven(ms, proj) if first and pair == 1 else proj + ms
    k = o.index(("m", u0 + 1, 2))
    o = o[:k] + [("mt", u0), ("mrow", u0), ("load_km", n0, 1)] + [("load_q", n0, 2)] * first + [("load_ke", n0, 1)] + o[k:]
    return o + [("load_q", n0, 2)] * (not first) + [("load_q", n0, 3)]


def beside_units(n, L):
    b = n - B * L
    more = b < B - 1
    at = {(s, i): [] for s in range(S) for i in range(8)}

    def place(first, steps):
        for k, x in enumerate(steps, first):
            at[k // 8, k % 8].append(x)

    if b > 0:
        place(AT["v"][L], [("v", n)])
    if more:
        place(AT["keys"][L], project(n + 1, 2))
        if b > 0:
            place(0, project(n + 1, 0)[2:])
            place(AT["queries"][L], project(n + 1, 1))
    if b > 0:
        place(AT["wo0"][L], parts(("wo", n - 1, 0)))
        place(AT["wo1"][L], parts(("wo", n - 1, 1)))
    if b + 2 < B:
        if n == 0:
            at[1, 4].append(("split", L, "attn", 3))
            at[2, 4].append(("split", L, "attn", 4))
        if b == 0:
            at[1, 0].append(("stats", L, 2))
            at[1, 2].append(("stats", L, 3))
            at[1, 5] += [("root", L, 2), ("root", L, 3)]
            at[1, 7] += [("rstd", L, 2), ("rstd", L, 3)]
        place(AT["ln"][L], [("ln", n + 2)])
        place(AT["xn"][L], transposed(n + 2))
        place(30, parts(("qkv", n + 2, 0))[:2])
    if not more:
        for at_, x in zip(AT["weights"][L], (("up", 0), ("up", 1), ("down", 0))):
            place(at_, [("split", L) + x])
        first, count = AT["hidden"][L]
        place(first, first_hidden(L)[:count])
    return at


def first_hidden(L):
    return parts(("up", L, 0)) + (parts(("up", L, 1)) if L == 0 else [])


def attention_order(L):
    n0, u0, u1 = B * L, B * S * L, B * S * (L + 1)
    o = []
    for u in range(u0, u1):
        n, s = divmod(u, S)
        b = n - n0
        more = b < B - 1
        if s == 0:
            beside = beside_units(n, L)
        for i in range(8):
            if i == 0:
                if s == 0 and b > 0:
                    o += [("load_ke", n, 1), ("load_q", n, 3)]
                if s > 1 and more:
                    o += [("load_q", n + 1, s - 1)]
                if s == 2 and more:
                    o += [("load_km", n + 1, 1), ("load_ke", n + 1, 0)]
                if s > 0 and not more:
                    o += [("load_xf", L, s - 1)]
            o += [("st", u, i)]
            if u + 2 < u1:
                o += [("m", u + 2, i)]
            if i == AT["pv1"][L] and u > u0:
                o += [("pv", u - 1, 1)]
            if i == AT["mt"][L] and u + 1 < u1:
                o += [("mt", u + 1), ("mrow", u + 1)]
            if i == 3 and s == 1 and more:
                o += [("load_km", n + 1, 0)]
            if i == 0 and s == 1 and more:
                o += [("load_q", n + 1, 0)]
            if 0 <= i - AT["norm"][L] < 4 and u > u0:
                o += [("norm", u - 1, i - AT["norm"][L])]
            if i == AT["pv0"][L]:
                o += [("pv", u, 0)]
            o += beside[s, i]
    o += [("load_xf", L, 3), ("pv", u1 - 1, 1)] + first_hidden(L)[AT["hidden"][L][1]:]
    o += [("norm", u1 - 1, k) for k in range(4)]
    o += [("hidden", L, 0), ("hidden_lo", L, 0), ("wo", n0 + B - 1, 0), ("wo", n0 + B - 1, 1)]
    return o + ([("up", L, 1)] if L == 1 else [])


def ffn_order(L):
    C = CHUNKS[L]
    first = 2 * C - BESIDE
    cut = L == 0
    o, late = [], []
    for c in range(2 * C + 1):
        part = []
        cut = L == 0 and c >= first
        if c < 2 * C:
            if c > 1:
                part += parts(("up", L, c)) if cut else [("up", L, c)]
            if c > 0:
                part += [("hidden", L, c)]
            if c + 2 < 2 * C:
                part += [("split", L, "up", c + 2)]
        if c >= 1:
            if (c - 1) % C == 0:
                part += [("bias", L, (c - 1) // C)]
            part += parts(("down", L, c - 1)) if cut else [("down", L, c - 1)]
            if c < 2 * C:
                part.insert(-2 if cut else len(part), ("hidden_lo", L, c))
            if (c - 1) % C == C - 1:
                h = (c - 1) // C
                part += [("add", L, h)]
                if L == 1:
                    part += [("out", h)]
        if c + 1 < 2 * C:
            part += [("split", L, "down", c + 1)]
        if L == 0 and C < c < C + 5:
            part += [(kind, 1, (c - C - 1) // 2) for kind in (("stats", "root"), ("rstd",))[(c - C - 1) % 2]]
        if L == 0 and c % 4 == 2 and c < 20:
            part += [("split", 1, "attn", c // 4)]
        if cut:
            late += part
        else:
            o += part
    if L == 0:
        start = attention_start(1)
        tail = [x for x in start if x[0] == "load_q" and x[2] > 1]
        o += woven(late, [x for x in start if x not in tail], early=EARLY) + tail
    return o


def program_order():
    o = [("stats", 0, 0), ("root", 0, 0), ("rstd", 0, 0)] + attention_start(0)
    for L in range(2):
        o += attention_order(L) + ffn_order(L)
    return o


def work_banks(order, wk):
    bank, before, last, taken = {}, {}, {}, set()
    beside, recent = False, [3, 4, 5, 7]
    for step in order:
        x = step[1] if step[0] == "part" else step
        if step[0] == "mt" and step[1] % (B * S) == B * S - 1:
            beside = True
        if step == ("st", B * S, 0):
            beside = False
        if x in wk and x not in bank:
            choice = (3, 4, 5) if not beside else (3,) if x[0] == "mt" and x[1] % (B * S) == B * S - 1 else (3, 7)
            k = [k for k in recent if k in choice and k not in taken][0]
            recent.remove(k)
            recent.append(k)
            bank[x], before[x] = k, last.get(k)
            last[k] = x
            taken.add(k)
        if step in wk and step[0] != "xn" and not direct(step) or \
                step[0] == "drain" and (step[1][0] == "xn" or direct(step[1])):
            x = step[1] if step[0] == "drain" else step
            taken.remove(bank[x])
            recent.remove(bank[x])
            recent.append(bank[x])
    return bank, before


def numbered(order, *kinds):
    return {x: k for k, x in enumerate(x for x in order if x[0] in kinds)}


def build(nc, x_in, attn_w, up_w, down_w, up_b, qkv_b, out_b, rope, out):
    order = program_order()
    wk = numbered(order, "m", "mt", "xn", "qkv", "v", "wo")
    em = {x: k for k, x in enumerate(x[1] if x[0] == "drain" else x for x in order
                                     if x[0] in ("m", "mt", "v", "wo") or x[0] == "drain" and (x[1][0] == "xn" or direct(x[1])))}
    qk = {x: k for k, x in enumerate(x for x in order if x[0] == "qkv" and not direct(x))}
    cp = numbered(order, "xn", "qkv")
    sp = numbered(order, "split")
    stg = numbered(order, "store")
    stt = numbered(order, "stats")
    ups = numbered(order, "up")
    downs = numbered(order, "down")
    adds = numbered(order, "add")
    bank_of, before = work_banks(order, wk)
    units_done, hidden_done, count = {}, {}, {"pv": 0, "hidden": 0}
    for x in order:
        if x[0] == "hidden" or x[0] == "pv" and x[2] == 1:
            count[x[0]] += 1
        y = x[1] if x[0] == "part" else x
        if y in wk and y not in units_done:
            units_done[y], hidden_done[y] = count["pv"], count["hidden"]
    in_parts = {x for x in order if x[0] == "part"}
    hips = {x: k for k, x in enumerate(x for x in order if x[0] == "qkv" and x[1] >= B)}

    qscr = nc.dram_tensor("q_parts", (2 * B, S, 2 * HD, UH * T), F32, kind="Internal").ap()
    kscr = nc.dram_tensor("k_parts", (2 * B, 4, HD, NKV * T), F32, kind="Internal").ap()
    xscr = nc.dram_tensor("xn_parts", (2, 2, P, 2 * KT, HALF), F32, kind="Internal").ap()

    with ExitStack() as ctx:
        def sb(name, shape, dt=F32):
            return ctx.enter_context(nc.sbuf_tensor(name, shape, dt))

        def sem(name):
            return ctx.enter_context(nc.semaphore(name))

        banks = ctx.enter_context(nc.psum_tensor("banks", [P, 8, 512], F32))
        x_res = sb("x_res", [P, NT, D])
        w_qkv = sb("w_qkv", [P, 2, 3, KT, 2 * P], F32R)
        w_out = sb("w_out", [P, 2, S, D], F32R)
        raw = sb("raw", [P, RAW, 1024])
        w_up = sb("w_up", [P, 2, 2, 1024], F32R)
        w_down = sb("w_down", [P, 2, 2, 512], F32R)
        xn = sb("xn", [P, TT, D])
        xnT = sb("xnT", [P, 2, KT, T], F32R)
        big = sb("big", [P, S, UH, T], F32R)
        k_max = sb("k_max", [ROWS, NKV, T], F32R)
        k_exp = sb("k_exp", [ROWS, NKV, T], F32R)
        v_t = sb("v_t", [P, T])
        v_sb = sb("v_sb", [P, TT, NKV, 2 * HD])
        stage = sb("stage", [P, 2, 2, 2, T], F32R)
        probs = sb("probs", [P, 8, 512])
        neg_max = sb("neg_max", [P, S, TT, UH])
        max_t = sb("max_t", [UH, 2, T], F32R)
        o_tok = sb("o_tok", [P, 2 * T])
        o_rec = sb("o_rec", [P, 16])
        o_div = sb("o_div", [P, T])
        o_t = sb("o_t", [P, T])
        ctxT = sb("ctxT", [P, 2, S, T], F32R)
        qkv_v = sb("qkv_v", [P, 2, T])
        rot_a = sb("rot_a", [P, 2, T])
        rot_b = sb("rot_b", [P, 2, T])
        table = sb("table", [P, 2, T])
        bias_qkv = sb("bias_qkv", [P, QKV // P])
        bias_up = sb("bias_up", [P, 24])
        bias_out = sb("bias_out", [P, 2, D], F32R)
        ones = sb("ones", [P, P], F32R)
        ident = sb("ident", [P, P])
        identb = sb("identb", [P, P], BF16)
        mask_qk = sb("mask_qk", [P, P], BF16)
        bn = sb("bn", [P, NT, 6])
        mv = sb("mv", [P, NT, 2])
        var_e = sb("var_e", [P, NT])
        dev = sb("dev", [P, NT])
        rs0 = sb("rs0", [P, NT])
        rs1 = sb("rs1", [P, NT])
        rstd = sb("rstd", [P, NT])

        hid = probs[:, :, :].rearrange("p (k s) t -> p k s t", k=4)
        hid_part = [[w_up[:, :, e, 512:1024] for e in range(2)],
                    [stage[:, :, e, :, :].rearrange("p k j t -> p k (j t)") for e in range(2)]]
        bias_raw = probs[:, 0:2, :]
        hid_f = hid[:, 0]
        gate_f = hid[:, 1]

        x_loaded = [sem(f"x_loaded{b}") for b in range(B)]
        bias_loaded = sem("bias_loaded")
        c_loaded = sem("c_loaded")
        made = sem("made")
        identb_made = sem("identb_made")
        bias_split = sem("bias_split")
        raw_loaded = [sem(f"raw_loaded{k}") for k in range(RAW)]
        hi_split = sem("hi_split")
        lo_split = sem("lo_split")
        var_ready = sem("var_ready")
        dev_ready = sem("dev_ready")
        stat_steps = sem("stat_steps")
        ln_done = sem("ln_done")
        wk_filled = sem("wk_filled")
        wk_copied = sem("wk_copied")
        wk_emptied = sem("wk_emptied")
        xn_stored = sem("xn_stored")
        staged = [sem(f"staged{k}") for k in range(2)]
        q_loaded = [sem(f"q_loaded{k}") for k in range(S)]
        km_loaded = [sem(f"km_loaded{k}") for k in range(2)]
        ke_loaded = [sem(f"ke_loaded{k}") for k in range(2)]
        m_loaded = [sem(f"m_loaded{k}") for k in range(S)]
        st_filled = sem("st_filled")
        exp_done = sem("exp_done")
        mask_done = sem("mask_done")
        pv_done = sem("pv_done")
        o_turned = sem("o_turned")
        o_inverted = sem("o_inverted")
        o_divided = sem("o_divided")
        o_back = sem("o_back")
        ctx_hi = sem("ctx_hi")
        ctx_lo = sem("ctx_lo")
        rot_cos = sem("rot_cos")
        rot_sin = sem("rot_sin")
        rot_done = sem("rot_done")
        rot_hi = sem("rot_hi")
        staged_lo = sem("staged_lo")
        xf_loaded = [sem(f"xf_loaded{k}") for k in range(2)]
        up_done = sem("up_done")
        hi_done = sem("hi_done")
        full_done = sem("full_done")
        gate_done = sem("gate_done")
        lo_done = sem("lo_done")
        down_done = sem("down_done")
        acc_filled = sem("acc_filled")
        added = sem("added")
        out_done = sem("out_done")

        def st_index(u, i):
            return 8 * u + i

        def unit(u):
            n, s = divmod(u, S)
            return n, s, s // 2

        def stores_in(layers, slot):
            return sum(k % 2 == slot for x, k in stg.items() if x[1] < B * layers)

        def work_bank(x):
            return bank_of[x]

        def wait_fill_read(eng, x):
            if x[0] == "qkv" and not direct(x):
                eng.wait_ge(wk_copied, cp[x] + 1)
            else:
                eng.wait_ge(wk_emptied, em[x] + 1)

        def last_fill(x, b):
            return [y for y in order[:order.index(x)] if bank_of.get(y) == b][-1]

        def stat_tiles(x):
            return range(TT * x[2], TT * x[2] + TT)

        def piece(L, what, k):
            if what == "attn":
                if k < 3:
                    to = [w_qkv[:, h, k, :, :] for h in range(2)]
                else:
                    to = [w_out[:, h, 2 * (k - 3):2 * (k - 3) + 2, :] for h in range(2)]
                return attn_w[L][:, k * 1024:(k + 1) * 1024], 1024, [y.rearrange("p k n -> p (k n)") for y in to]
            c = k % CHUNKS[L]
            if what == "up":
                n = 512 * (L + 1)
                return up_w[L][c], n, [w_up[:, k % 2, h, 0:n] for h in range(2)]
            return down_w[L][c], 512, [w_down[:, k % 2, h, :] for h in range(2)]

        def wait_weights_free(eng, L, what, k):
            if what == "attn" and L == 1:
                eng.wait_ge(wk_filled, wk[("wo", B - 1, 1)] + 1)
            if what == "up" and L == 1 and k < 2:
                eng.wait_ge(down_done, 2 * CHUNKS[0])
            if what == "up" and ups[("up", L, k)] >= 2:
                eng.wait_ge(up_done, ups[("up", L, k)] - 1)
            if what == "down" and downs[("down", L, k)] >= 2:
                eng.wait_ge(down_done, downs[("down", L, k)] - 1)

        IDENT, ZEROED, ONES_V, M_ROWS, ALL_MADE = 2, 3, 5, 6, 11

        block = ctx.enter_context(nc.Block())

        @block.sync
        def _(sp_):
            def load_x(b):
                sp_.dma_start(x_res[:, TT * b:TT * b + TT, :],
                              x_in[b].rearrange("(t p) d -> p t d", p=P)).then_inc(x_loaded[b], 16)

            load_x(0)
            sp_.wait_ge(raw_loaded[0], 16)
            load_x(1)
            sp_.wait_ge(made, ZEROED)
            for row in (0, 32):
                sp_.dma_start(bias_raw[row:row + 2, :, :], out_b).then_inc(bias_loaded, 16)
            for x in order:
                if x[0] == "store_xn":
                    n = x[1]
                    L, b = divmod(n, B)
                    sp_.wait_ge(wk_emptied, em[("xn", n, 1)] + 1)
                    if n >= 1:
                        sp_.wait_ge(xn_stored, 16 * n)
                    sp_.dma_start(xscr[L, b // 2, :, :, (b % 2) * T:(b % 2) * T + T],
                                  xnT[:, :, :, :].rearrange("p h k t -> p (h k) t").bitcast(F32)).then_inc(xn_stored, 16)
                if x[0] == "store":
                    _, n, pair = x
                    k = stg[x]
                    if direct(("qkv", n, pair)):
                        sp_.wait_ge(wk_emptied, em[("qkv", n, pair)] + 1)
                    else:
                        sp_.wait_ge(staged_lo, qk[("qkv", n, pair)] + 1)
                    if pair < 2:
                        for j in range(2):
                            dst = qscr[n, 2 * pair + j].rearrange("(h d) (g t) -> (d g) h t", h=2, g=UH)
                            sp_.dma_start(dst, stage[:, k % 2, :, j, :].bitcast(F32)).then_inc(staged[k % 2], 16)
                    else:
                        for j in range(2):
                            dst = kscr[n].rearrange("(h e) d (g t) -> e (d g) h t", e=2, g=NKV)[j]
                            sp_.dma_start(dst, stage[:, k % 2, :, 0, :].bitcast(F32)).then_inc(staged[k % 2], 16)
                if x[0] == "load_q":
                    _, n, s = x
                    k = stg[("store", n, s // 2)]
                    sp_.wait_ge(staged[k % 2], 32 * (k // 2 + 1))
                    if n % B:
                        sp_.wait_ge(st_filled, st_index(S * (n - 1) + s, 7) + 1)
                    elif n:
                        sp_.wait_ge(up_done, ups[("up", 0, (s // 2 + 1) * CHUNKS[0] - 1)] + 1)
                    for e in range(2):
                        sp_.dma_start(big[32 * e:32 * e + 32, s, :, :].rearrange("p g t -> p (g t)").bitcast(F32),
                                      qscr[n, s]).then_inc(q_loaded[s], 16)
                if x[0] in ("load_km", "load_ke"):
                    kind, n, f = x
                    k = stg[("store", n, 2)]
                    sp_.wait_ge(staged[k % 2], 32 * (k // 2 + 1))
                    g = slice(4 * f * T, (4 * f + 4) * T)
                    buf, done = (k_max, km_loaded[f]) if kind == "load_km" else (k_exp, ke_loaded[f])
                    if n and kind == "load_km":
                        sp_.wait_ge(wk_filled, wk[("m", S * (n - 1) + 2 * f + 1, 7)] + 1)
                    elif n:
                        sp_.wait_ge(st_filled, st_index(S * (n - 1) + 2 * f + 1, 7) + 1)
                    sp_.dma_start(buf[0:4 * HD, 4 * f:4 * f + 4, :].rearrange("p g t -> p (g t)").bitcast(F32),
                                  kscr[n].rearrange("q d x -> (q d) x")[:, g]).then_inc(done, 16)
                if x[0] == "mrow":
                    u = x[1]
                    n, s, f = unit(u)
                    sp_.wait_ge(wk_emptied, em[("mt", u)] + 1)
                    sp_.dma_start(big[MROW:MROW + 1, s, :, :].bitcast(F32),
                                  max_t[:, u % 2, :].bitcast(F32)).then_inc(m_loaded[s], 16)
                    if u == 1:
                        load_x(2)
                        load_x(3)
                        for dst, src in ((table[:, :, :], rope), (bias_qkv[:, :], qkv_b), (bias_up[:, :], up_b)):
                            sp_.dma_start(dst, src).then_inc(c_loaded, 16)
                if x[0] == "load_xf":
                    _, L, e = x
                    h, part = divmod(e, 2)
                    sp_.wait_ge(xn_stored, 16 * B * (L + 1))
                    sp_.wait_ge(st_filled, st_index(S * (B * L + B - 1) + e, 7) + 1)
                    for rows in (slice(0, 64), slice(64, P)):
                        sp_.dma_start(big[rows, e, :, :].rearrange("p g t -> p (g t)").bitcast(F32),
                                      xscr[L, h, rows, part * KT:part * KT + KT].rearrange("p k t -> p (k t)")
                                      ).then_inc(xf_loaded[h], 16)
                if x[0] == "out":
                    h = x[1]
                    for t in range(HT):
                        tile = HT * h + t
                        sp_.wait_ge(added, 4 * adds[("add", 1, h)] + t + 1)
                        sp_.dma_start(out[tile // TT, (tile % TT) * P:(tile % TT) * P + P, :],
                                      x_res[:, tile, :]).then_inc(out_done, 16)
            sp_.wait_ge(out_done, 16 * NT)

        @block.gpsimd
        def _(pool):
            def load(k, x):
                src, n, _ = piece(*x[1:])
                pool.dma_start(raw[:, k % RAW, 0:n], src).then_inc(raw_loaded[k % RAW], 16)

            pieces = [x for x in order if x[0] == "split"]
            load(0, pieces[0])
            pool.wait_ge(x_loaded[0], 16)
            load(1, pieces[1])
            nc.gpsimd.memset(ident[:, :], 0.0).then_inc(made, 1)
            pool.wait_ge(made, 1)
            nc.gpsimd.affine_select(out=ident[:, :], in_=ident[:, :], compare_op=ALU.not_equal, fill=1.0,
                                    base=0, pattern=[[-1, P]], channel_multiplier=1).then_inc(made, 1)
            pool.wait_ge(made, IDENT)
            pool.wait_ge(raw_loaded[0], 16)
            load(2, pieces[2])
            nc.gpsimd.memset(bias_raw[:, :, :], 0.0).then_inc(made, 1)
            pool.wait_ge(made, ZEROED)
            nc.gpsimd.memset(k_max[64:ROWS, :, :].bitcast(F32), 0.0).then_inc(made, 1)
            pool.wait_ge(made, 4)
            nc.gpsimd.memset(v_sb[:, :, :, :], 1.0).then_inc(made, 1)
            pool.wait_ge(made, ONES_V)
            nc.gpsimd.memset(big[64:ROWS, :, :, :].bitcast(F32), 0.0).then_inc(made, 1)
            pool.wait_ge(made, M_ROWS)
            nc.gpsimd.memset(k_exp[64:ROWS, :, :].bitcast(F32), 0.0).then_inc(made, 1)
            pool.wait_ge(made, 7)
            nc.gpsimd.memset(k_exp[MROW:MROW + 1, :, :].bitcast(F32), 1.0).then_inc(made, 1)
            pool.wait_ge(made, 8)
            nc.gpsimd.memset(ones[:, :].bitcast(F32), 1.0).then_inc(made, 1)
            pool.wait_ge(made, 9)
            nc.gpsimd.memset(mask_qk[:, :], 0.0).then_inc(made, 1)
            pool.wait_ge(made, 10)
            nc.gpsimd.affine_select(out=mask_qk[:, :], in_=mask_qk[:, :], compare_op=ALU.is_ge, fill=MASKED,
                                    base=0, pattern=[[-1, P]], channel_multiplier=1).then_inc(made, 1)
            pool.wait_ge(made, ALL_MADE)
            last = [(made, ALL_MADE)]

            def in_order():
                pool.wait_ge(*last[0])

            for x in order:
                if x[0] == "st" and x[1] >= B * S:
                    _, u, i = x
                    slot = probs[:, i, 0:512 if i < 4 else 2 * P].rearrange("p (r t) -> p r t", r=2)[:, :, 0:P]
                    pool.wait_ge(exp_done, st_index(u, i) + 1)
                    in_order()
                    nc.gpsimd.affine_select(out=slot, in_=slot, compare_op=ALU.is_ge, fill=0.0, base=0,
                                            pattern=[[0, 2], [1, P]], channel_multiplier=-1).then_inc(mask_done, 1)
                    last[0] = (mask_done, st_index(u - B * S, i) + 1)
                if x == ("mrow", 0):
                    pool.wait_ge(lo_split, RAW)
                    pool.wait_ge(m_loaded[0], 16)
                    for k in range(RAW, 2 * RAW):
                        load(k, pieces[k])
                if x[0] == "split" and RAW <= sp[x] < len(pieces) - RAW:
                    pool.wait_ge(lo_split, sp[x] + 1)
                    load(sp[x] + RAW, pieces[sp[x] + RAW])
                if x[0] == "norm" and x[2] == 3:
                    u = x[1]
                    n, s, f = unit(u)
                    pool.wait_ge(ctx_hi, u + 1)
                    in_order()
                    nc.gpsimd.tensor_tensor(ctxT[:, 1, s, :], o_t[:, :], ctxT[:, 0, s, :].bitcast(F32),
                                            ALU.subtract).then_inc(ctx_lo, 1)
                    last[0] = (ctx_lo, u + 1)
                if x[0] == "qkv" and x[1] >= B:
                    _, n, pair = x
                    w = 2 if pair < 2 else 1
                    k = stg[("store", n, pair)]
                    pool.wait_ge(wk_copied, cp[x] + 1)
                    if hips[x]:
                        pool.wait_ge(rot_done, hips[x])
                    in_order()
                    nc.gpsimd.tensor_tensor(rot_a[:, 0:w, :], qkv_v[:, 0:w, :],
                                            table[:, 0:1, :].to_broadcast([P, w, T]), ALU.mult).then_inc(rot_cos, 1)
                    last[0] = (rot_cos, hips[x] + 1)
                if x[0] == "drain" and x[1] in qk and x[1][1] < B:
                    x = x[1]
                    _, n, pair = x
                    w = 2 if pair < 2 else 1
                    k = stg[("store", n, pair)]
                    pool.wait_ge(wk_copied, cp[x] + 1)
                    in_order()
                    nc.gpsimd.tensor_tensor(stage[:, k % 2, 1, 0:w, :], qkv_v[:, 0:w, :],
                                            stage[:, k % 2, 0, 0:w, :].bitcast(F32), ALU.subtract).then_inc(staged_lo, 1)
                    last[0] = (staged_lo, qk[x] + 1)
                if x[0] == "round":
                    x = x[1]
                    _, n, pair = x
                    w = 2 if pair < 2 else 1
                    k = stg[("store", n, pair)]
                    pool.wait_ge(rot_hi, hips[x] + 1)
                    in_order()
                    nc.gpsimd.tensor_tensor(stage[:, k % 2, 1, 0:w, :], rot_b[:, 0:w, :],
                                            stage[:, k % 2, 0, 0:w, :].bitcast(F32), ALU.subtract).then_inc(staged_lo, 1)
                    last[0] = (staged_lo, qk[x] + 1)

        @block.tensor
        def _(pe):
            def work(x):
                k, y = bank_of[x], before[x]
                if y:
                    wait_fill_read(pe, y)
                if k == 7 and (not y or units_done[x] > units_done[y]):
                    pe.wait_ge(o_turned, units_done[x])
                if k in (4, 5) and y and hidden_done[x] > hidden_done[y]:
                    pe.wait_ge(lo_done, hidden_done[x])
                return k

            def three(out_ap, lhs, rhs, first, last, **kw):
                for j, (a, b_) in enumerate(((0, 0), (1, 0), (0, 1))):
                    mm = nc.tensor.matmul(out_ap, lhs(a), rhs(b_), start=first and j == 0, stop=last and j == 2, **kw)
                return mm

            pe.wait_ge(made, IDENT)
            for step in order:
                x = step[1] if step[0] == "part" else step
                count = len(parts(x)) if x[0] in ("qkv", "wo", "up", "down") else 1
                cut = ("part", x, 0) in in_parts
                part = step[2] if step[0] == "part" else count - 1 if cut else None
                opens, closes = part in (0, None), part in (count - 1, None)

                def mine(groups):
                    w = len(groups) // count
                    return groups if part is None else groups[part * w:part * w + w]

                if x[0] == "xn":
                    _, n, t = x
                    k = work(x)
                    pe.wait_ge(ln_done, TT * n + t + 1)
                    for c in range(KT):
                        mm = nc.tensor.transpose(banks[:, k, c * P:c * P + P], xn[:, t, c * P:c * P + P], ident[:, :])
                    mm.then_inc(wk_filled, 1)
                if x[0] == "qkv":
                    _, n, pair = x
                    k = work(x) if opens else work_bank(x)
                    if opens:
                        pe.wait_ge(wk_emptied, em[("xn", n, 1)] + 1)
                        pe.wait_ge(lo_split, sp[("split", n // B, "attn", pair)] + 1)
                    for j, c in mine([(j, c) for j in range(2) for c in range(KT)]):
                        mm = three(banks[:, k, j * T:j * T + T],
                                   lambda h: w_qkv[:, h, pair, c, j * P:j * P + P], lambda h: xnT[:, h, c, :],
                                   c == 0, c == KT - 1)
                    if closes:
                        mm.then_inc(wk_filled, 1)
                if x[0] == "v":
                    n = x[1]
                    k = work(x)
                    pe.wait_ge(wk_copied, cp[("qkv", n, 2)] + 1)
                    for t in range(TT):
                        mm = nc.tensor.transpose(banks[:, k, t * P:t * P + P], v_t[:, t * P:t * P + P], ident[:, :])
                    mm.then_inc(wk_filled, 1)
                if x[0] == "m":
                    _, u, i = x
                    n, s, f = unit(u)
                    t, g = divmod(i, 4)
                    k = work(x)
                    if x == ("m", 0, 0):
                        pe.wait_ge(made, M_ROWS)
                    if x == ("m", B * S, 0):
                        pe.wait_ge(identb_made, 1)
                    if i == 0:
                        pe.wait_ge(q_loaded[s], 32 * (n + 1))
                        pe.wait_ge(km_loaded[f], 16 * (n + 1))
                    for r in range(2):
                        mm = nc.tensor.matmul(banks[:, k, r * T:r * T + T],
                                              big[0:ROWS, s, 2 * g + r, t * P:t * P + P], k_max[0:ROWS, 4 * f + g, :],
                                              start=r == 0, stop=n < B and r == 1, skip_group_check=True)
                    if n >= B:
                        diagonal = banks[:, k, :].rearrange("p (r t) -> p r t", r=2)[:, :, t * P:t * P + P]
                        mm = nc.tensor.matmul(diagonal, identb[:, :], mask_qk[:, None, :].to_broadcast([P, 2, P]),
                                              start=False, stop=True, skip_group_check=True)
                    mm.then_inc(wk_filled, 1)
                if x[0] == "mt":
                    u = x[1]
                    n, s, f = unit(u)
                    k = work(x)
                    pe.wait_ge(wk_emptied, em[("m", u, 7)] + 1)
                    for t in range(TT):
                        mm = nc.tensor.transpose(banks[0:UH, k, t * P:t * P + P], neg_max[:, s, t, :], ident[:, :])
                    mm.then_inc(wk_filled, 1)
                if x[0] == "st":
                    _, u, i = x
                    n, s, f = unit(u)
                    t, g = divmod(i, 4)
                    k = st_index(u, i)
                    if k >= 3:
                        pe.wait_ge(exp_done, k - 2)
                    if k == 0:
                        pe.wait_ge(made, ALL_MADE)
                    if x == ("st", B * S, 0):
                        pe.wait_ge(added, NT - 1)
                    if i == 0:
                        pe.wait_ge(m_loaded[s], 16 * (n + 1))
                        pe.wait_ge(ke_loaded[f], 16 * (n + 1))
                    keys = k_exp[0:ROWS, 4 * f + g, t * P:t * P + P]
                    bank = banks[:, k % 3, :].rearrange("p (r t) -> p r t", r=2)
                    if n < B:
                        mm = nc.tensor.matmul(bank, keys, big[0:ROWS, s, 2 * g:2 * g + 2, :], start=True, stop=True)
                    else:
                        q0 = t * P
                        part = bank if t == 0 else banks[:, k % 3, 0:2 * P].rearrange("p (r t) -> p r t", r=2)
                        mm = nc.tensor.matmul(part, keys, big[0:ROWS, s, 2 * g:2 * g + 2, q0:], start=True, stop=True)
                    mm.then_inc(st_filled, 1)
                if x[0] == "pv":
                    _, u, t = x
                    n, s, f = unit(u)
                    if n < B:
                        pe.wait_ge(exp_done, st_index(u, 4 * t + 3) + 1)
                    else:
                        pe.wait_ge(mask_done, st_index(u - B * S, 4 * t + 3) + 1)
                    if t == 0 and u >= 2:
                        pe.wait_ge(o_turned, u - 1)
                    if x == ("pv", B * S, 0):
                        pe.wait_ge(added, NT)
                    if x == ("pv", B * S + 1, 0):
                        wait_fill_read(pe, last_fill(x, 7))
                    if t == 0 and s == 0:
                        pe.wait_ge(wk_emptied, em[("v", n)] + 1)
                    for g in range(4):
                        o = banks[32 * g:32 * g + 32, 6 + u % 2, :]
                        p_ = probs[:, 4 * t + g, :]
                        if n >= B and t == 1:
                            o = o.rearrange("p (r t) -> p r t", r=2)[:, :, P:2 * P]
                            p_ = p_[:, 0:2 * P].rearrange("p (r t) -> p r t", r=2)
                        mm = nc.tensor.matmul(o, v_sb[:, t, 4 * f + g, :], p_, start=t == 0, stop=t == 1,
                                              skip_group_check=True)
                    mm.then_inc(pv_done, 1)
                if x[0] == "wo":
                    _, n, t = x
                    k = work(x) if opens else work_bank(x)
                    if opens:
                        pe.wait_ge(ctx_lo, S * (n + 1))
                        pe.wait_ge(lo_split, sp[("split", n // B, "attn", 4)] + 1)
                    for s in mine(range(S)):
                        mm = three(banks[:, k, :], lambda h: ctxT[:, h, s, t * P:t * P + P],
                                   lambda h: w_out[:, h, s, :], s == 0, s == S - 1)
                    if closes:
                        mm.then_inc(wk_filled, 1)
                if x[0] == "up":
                    _, L, c = x
                    h = c // CHUNKS[L]
                    hid_banks = [HID[c % 2]] if L == 0 else [HID[2 * (c % 2)], HID[2 * (c % 2) + 1]]
                    if opens:
                        pe.wait_ge(lo_split, sp[("split", L, "up", c)] + 1)
                        if c % CHUNKS[L] == 0:
                            pe.wait_ge(xf_loaded[h], 64 * (L + 1))
                        if c < 2:
                            for k in hid_banks:
                                wait_fill_read(pe, last_fill(x, k))
                            if 7 in hid_banks:
                                pe.wait_ge(o_turned, B * S * (L + 1))
                        else:
                            pe.wait_ge(lo_done, ups[x] - 1)
                    xf = big[:, 2 * h:2 * h + 2, :, :].rearrange("p a g t -> p (a g t)").rearrange(
                        "p (h k t) -> p h k t", h=2, k=KT)
                    for j, q in mine([(j, q) for j in range(L + 1) for q in range(KT)]):
                        mm = three(banks[:, hid_banks[j], :],
                                   lambda e: w_up[:, c % 2, e, (j * KT + q) * P:(j * KT + q) * P + P],
                                   lambda e: xf[:, e, q, :], q == 0, q == KT - 1)
                    if closes:
                        mm.then_inc(up_done, 1)
                if x[0] == "bias":
                    _, L, h = x
                    if h == 0:
                        pe.wait_ge(exp_done, 8 * B * S * (L + 1))
                        pe.wait_ge(o_turned, B * S * (L + 1))
                    pe.wait_ge(bias_split, 1)
                    for t in range(HT):
                        if h == 1:
                            pe.wait_ge(added, HT * 2 * L + t + 1)
                        nc.tensor.matmul(banks[:, ACC[t], :], ones[:, :], bias_out[:, L, :],
                                         start=True, stop=False, skip_group_check=True)
                if x[0] == "down":
                    _, L, c = x
                    if opens:
                        pe.wait_ge(lo_split, sp[("split", L, "down", c)] + 1)
                        pe.wait_ge(lo_done, downs[x] + 1)
                    for t in mine(range(HT)):
                        mm = three(banks[:, ACC[t], :], lambda h: hid_part[L][h][:, c % 2, t * P:t * P + P],
                                   lambda h: w_down[:, c % 2, h, :], False, c % CHUNKS[L] == CHUNKS[L] - 1,
                                   skip_group_check=True)
                        if c % CHUNKS[L] == CHUNKS[L] - 1 and t < HT - 1:
                            mm.then_inc(acc_filled, 1)
                    if closes:
                        mm.then_inc(down_done, 1)

        @block.scalar
        def _(act):
            copies = 0
            for x in order:
                if x[0] == "split":
                    k = sp[x]
                    _, n, to = piece(*x[1:])
                    act.wait_ge(raw_loaded[k % RAW], 16 * (k // RAW + 1))
                    wait_weights_free(act, *x[1:])
                    nc.scalar.copy(to[0], raw[:, k % RAW, 0:n]).then_inc(hi_split, 1)
                if x[0] == "root":
                    k = stt[("stats",) + x[1:]]
                    tiles = stat_tiles(x)
                    t = slice(tiles[0], tiles[-1] + 1)
                    act.wait_ge(var_ready, k + 1)
                    nc.scalar.activation(dev[:, t], var_e[:, t], ACT.Sqrt).then_inc(dev_ready, 1)
                if x[0] == "xn":
                    _, n, t = x
                    act.wait_ge(wk_filled, wk[x] + 1)
                    if n and t == 0:
                        act.wait_ge(wk_filled, max(wk[("qkv", n - 1, j)] for j in range(3)) + 1)
                        act.wait_ge(xn_stored, 16 * n)
                    nc.scalar.copy(xnT[:, 0, :, t * P:t * P + P],
                                   banks[:, work_bank(x), :].rearrange("p (k t) -> p k t", k=KT)).then_inc(wk_copied, 1)
                if x[0] == "qkv":
                    _, n, pair = x
                    k = stg[("store", n, pair)]
                    w = 2 if pair < 2 else 1
                    bank = banks[:, work_bank(x), :].rearrange("p (j t) -> p j t", j=2)
                    act.wait_ge(wk_filled, wk[x] + 1)
                    if n < B:
                        if k >= 2:
                            act.wait_ge(staged[k % 2], 32 * (k // 2))
                        ins = nc.scalar.copy(stage[:, k % 2, 0, 0:w, :], bank[:, 0:w, :])
                        if qk.get(x):
                            act.wait_ge(staged_lo, qk[x])
                        if x in qk:
                            ins = nc.scalar.copy(qkv_v[:, 0:w, :], bank[:, 0:w, :])
                    else:
                        if hips[x]:
                            act.wait_ge(rot_cos, hips[x])
                            act.wait_ge(rot_done, hips[x])
                        else:
                            act.wait_ge(staged_lo, qk[x])
                        for j in range(w):
                            ins = nc.scalar.activation(qkv_v[:, j, :], bank[:, j, :], ACT.Identity,
                                                       bias=bias_qkv[:, 2 * pair + j:2 * pair + j + 1])
                    if pair == 2:
                        if n % B:
                            act.wait_ge(wk_filled, wk[("v", n - 1)] + 1)
                        elif n:
                            act.wait_ge(wk_filled, wk[("v", n - 1)] + 1)
                        if n < B:
                            ins = nc.scalar.copy(v_t[:, :], bank[:, 1, :])
                        else:
                            ins = nc.scalar.activation(v_t[:, :], bank[:, 1, :], ACT.Identity, bias=bias_qkv[:, 5:6])
                    ins.then_inc(wk_copied, 1)
                if x[0] == "round":
                    x = x[1]
                    _, n, pair = x
                    k = stg[("store", n, pair)]
                    w = 2 if pair < 2 else 1
                    act.wait_ge(rot_done, hips[x] + 1)
                    act.wait_ge(staged[k % 2], 32 * (k // 2))
                    nc.scalar.copy(stage[:, k % 2, 0, 0:w, :], rot_b[:, 0:w, :]).then_inc(rot_hi, 1)
                if x[0] == "st":
                    _, u, i = x
                    n, s, f = unit(u)
                    t = i // 4
                    k = st_index(u, i)
                    act.wait_ge(st_filled, k + 1)
                    if k == 0:
                        act.wait_ge(bias_split, 1)
                    if x == ("st", B * S, 0):
                        act.wait_ge(lo_done, 2 * CHUNKS[0])
                    if u:
                        act.wait_ge(pv_done, 2 * (u - 1) + t + 1)
                    w = 2 * P if n >= B and t == 1 else 512
                    nc.scalar.activation(probs[:, i, 0:w], banks[:, k % 3, 0:w], ACT.Exp,
                                         scale=SCALES[n // B]).then_inc(exp_done, 1)
                if x[0] == "norm" and x[2] == 3:
                    u = x[1]
                    n, s, f = unit(u)
                    act.wait_ge(o_back, u + 1)
                    if n and s == 0:
                        act.wait_ge(wk_filled, wk[("wo", n - 1, 1)] + 1)
                    nc.scalar.copy(ctxT[:, 0, s, :], o_t[:, :]).then_inc(ctx_hi, 1)
                if x[0] == "hidden":
                    _, L, c = x
                    k = ups[("up", L, c)]
                    hid_hi = hid_part[L][0]
                    act.wait_ge(up_done, k + 1)
                    act.wait_ge(c_loaded, 48)
                    cc = c % CHUNKS[L]
                    if c == 0:
                        act.wait_ge(pv_done, 2 * B * S * (L + 1) - 1)
                    if c == 0 and L == 1:
                        for e in range(2):
                            act.wait_ge(staged[e], 32 * stores_in(L + 1, e))
                    if L == 0:
                        bias = bias_up[:, cc:cc + 1]
                        if k >= 2:
                            act.wait_ge(down_done, k - 1)
                            act.wait_ge(lo_done, k - 1)
                        nc.scalar.activation(hid_hi[:, c % 2, :], banks[:, HID[c % 2], :], ACT.Gelu_apprx_tanh,
                                             bias=bias).then_inc(hi_done, 1)
                        nc.scalar.activation(hid_f[:, c % 2, :], banks[:, HID[c % 2], :], ACT.Gelu_apprx_tanh,
                                             bias=bias).then_inc(full_done, 1)
                    else:
                        act.wait_ge(lo_done, k - 1)
                        nc.scalar.activation(gate_f[:, c % 2, :], banks[:, HID[2 * (c % 2)], :], ACT.Silu,
                                             bias=bias_up[:, 16 + cc:17 + cc]).then_inc(gate_done, 1)
                        act.wait_ge(full_done, k + 1)
                        act.wait_ge(down_done, k - 1)
                        nc.scalar.copy(hid_hi[:, c % 2, :], hid_f[:, c % 2, :]).then_inc(hi_done, 1)

        @block.vector
        def _(dve):
            steps = [0]

            def link(ins):
                steps[0] += 1
                ins.then_inc(stat_steps, 1)
                dve.wait_ge(stat_steps, steps[0])

            for x in order:
                if x[0] == "split":
                    k = sp[x]
                    _, n, to = piece(*x[1:])
                    dve.wait_ge(hi_split, k + 1)
                    nc.vector.tensor_tensor(to[1], raw[:, k % RAW, 0:n], to[0].bitcast(F32),
                                            ALU.subtract).then_inc(lo_split, 1)
                if x[0] == "stats":
                    _, L, b = x
                    tiles = stat_tiles(x)
                    for t in tiles:
                        if L == 0:
                            dve.wait_ge(x_loaded[t // TT], 16)
                        else:
                            dve.wait_ge(added, t + 1)
                        ins = nc.vector.bn_stats(bn[:, t, :], x_res[:, t, :])
                        link(ins)
                        ins = nc.vector.bn_aggr(mv[:, t, :], bn[:, t, :])
                    link(ins)
                    t = slice(tiles[0], tiles[-1] + 1)
                    nc.vector.tensor_scalar(var_e[:, t], mv[:, t, 1], EPS, None, ALU.add).then_inc(var_ready, 1)
                if x[0] == "rstd":
                    k = stt[("stats",) + x[1:]]
                    tiles = stat_tiles(x)
                    t = slice(tiles[0], tiles[-1] + 1)
                    dve.wait_ge(dev_ready, k + 1)
                    link(nc.vector.reciprocal(rs0[:, t], dev[:, t]))
                    link(nc.vector.tensor_tensor(rs1[:, t], rs0[:, t], rs0[:, t], ALU.mult))
                    link(nc.vector.tensor_tensor(rs1[:, t], rs1[:, t], var_e[:, t], ALU.mult))
                    link(nc.vector.tensor_scalar(rs1[:, t], rs1[:, t], -0.5, 1.5, ALU.mult, ALU.add))
                    link(nc.vector.tensor_tensor(rstd[:, t], rs0[:, t], rs1[:, t], ALU.mult))
                if x[0] == "ln":
                    n = x[1]
                    for t in range(TT):
                        tile = TT * (n % B) + t
                        if n:
                            dve.wait_ge(wk_filled, wk[("xn", n - 1, t)] + 1)
                        nc.vector.tensor_scalar(xn[:, t, :], x_res[:, tile, :], mv[:, tile, 0:1], rstd[:, tile:tile + 1],
                                                ALU.subtract, ALU.mult).then_inc(ln_done, 1)
                if x[0] == "drain" and x[1][0] == "xn":
                    x = x[1]
                    _, n, t = x
                    dve.wait_ge(wk_copied, cp[x] + 1)
                    nc.vector.tensor_tensor(xnT[:, 1, :, t * P:t * P + P],
                                            banks[:, work_bank(x), :].rearrange("p (k t) -> p k t", k=KT),
                                            xnT[:, 0, :, t * P:t * P + P].bitcast(F32), ALU.subtract).then_inc(wk_emptied, 1)
                if x[0] == "drain" and direct(x[1]):
                    x = x[1]
                    _, n, pair = x
                    k = stg[("store", n, pair)]
                    w = 2 if pair < 2 else 1
                    dve.wait_ge(wk_copied, cp[x] + 1)
                    bank = banks[:, work_bank(x), :].rearrange("p (j t) -> p j t", j=2)
                    nc.vector.tensor_tensor(stage[:, k % 2, 1, 0:w, :], bank[:, 0:w, :],
                                            stage[:, k % 2, 0, 0:w, :].bitcast(F32), ALU.subtract).then_inc(wk_emptied, 1)
                if x[0] == "drain" and x[1][0] == "qkv" and x[1][1] >= B:
                    x = x[1]
                    _, n, pair = x
                    w = 2 if pair < 2 else 1
                    dve.wait_ge(wk_copied, cp[x] + 1)
                    dve.wait_ge(c_loaded, 48)
                    dve.wait_ge(staged_lo, qk[x])
                    other = table[:, 1:2, :]
                    nc.vector.tensor_tensor(rot_b[0:64, 0:w, :], qkv_v[64:P, 0:w, :],
                                            other[64:P].to_broadcast([64, w, T]), ALU.mult).then_inc(rot_sin, 1)
                    nc.vector.tensor_tensor(rot_b[64:P, 0:w, :], qkv_v[0:64, 0:w, :],
                                            other[0:64].to_broadcast([64, w, T]), ALU.mult).then_inc(rot_sin, 1)
                    dve.wait_ge(rot_sin, 2 * hips[x] + 2)
                    dve.wait_ge(rot_cos, hips[x] + 1)
                    nc.vector.tensor_tensor(rot_b[:, 0:w, :], rot_b[:, 0:w, :], rot_a[:, 0:w, :],
                                            ALU.add).then_inc(rot_done, 1)
                if x[0] == "v":
                    n = x[1]
                    dve.wait_ge(wk_filled, wk[x] + 1)
                    if n == 0:
                        nc.vector.tensor_copy(identb[:, :], ident[:, :]).then_inc(identb_made, 1)
                        dve.wait_ge(bias_loaded, 32)
                        link(nc.vector.tensor_copy(bias_out[:, :, :], bias_raw[:, :, :]))
                        nc.vector.tensor_tensor(bias_out[32:64, :, :], bias_raw[32:64, :, :],
                                                bias_out[32:64, :, :].bitcast(F32), ALU.subtract).then_inc(bias_split, 1)
                        dve.wait_ge(made, ONES_V)
                    if n:
                        dve.wait_ge(pv_done, 2 * S * n)
                    nc.vector.tensor_copy(v_sb[:, :, :, 0:HD],
                                          banks[:, work_bank(x), 0:TT * P].rearrange("p (t g d) -> p t g d", t=TT, g=NKV)
                                          ).then_inc(wk_emptied, 1)
                if x[0] == "m":
                    _, u, i = x
                    n, s, f = unit(u)
                    t, g = divmod(i, 4)
                    dve.wait_ge(wk_filled, wk[x] + 1)
                    if n:
                        dve.wait_ge(wk_filled, wk[("mt", u - S)] + 1)
                    w = T if n < B or t == 1 else P
                    nc.vector.tensor_reduce(neg_max[:, s, t, 2 * g:2 * g + 2],
                                            banks[:, work_bank(x), :].rearrange("p (r t) -> p r t", r=2)[:, :, 0:w],
                                            AX.X, ALU.max, negate=True).then_inc(wk_emptied, 1)
                if x[0] == "mt":
                    u = x[1]
                    n, s, f = unit(u)
                    dve.wait_ge(wk_filled, wk[x] + 1)
                    if u >= 2:
                        dve.wait_ge(m_loaded[(u - 2) % S], 16 * ((u - 2) // S + 1))
                    nc.vector.tensor_copy(max_t[:, u % 2, :], banks[0:UH, work_bank(x), 0:T]).then_inc(wk_emptied, 1)
                if x[0] == "norm":
                    _, u, k = x
                    if k == 0:
                        dve.wait_ge(pv_done, 2 * u + 2)
                        if u:
                            dve.wait_ge(o_divided, u)
                        nc.vector.transpose(o_tok[:, :], banks[:, 6 + u % 2, :]).then_inc(o_turned, 1)
                    by = o_tok[:, :].rearrange("p (r q c) -> p r q c", r=2, q=8)
                    if k == 1:
                        dve.wait_ge(o_turned, u + 1)
                        nc.vector.reciprocal(o_rec[:, :].rearrange("p (r q) -> p r q", r=2), by[:, :, :, HD]).then_inc(o_inverted, 1)
                    if k == 2:
                        dve.wait_ge(o_inverted, u + 1)
                        if u:
                            dve.wait_ge(o_back, u)
                        nc.vector.tensor_tensor(o_div[:, :].rearrange("p (q r c) -> p r q c", r=2, c=HD), by[:, :, :, 0:HD],
                                                o_rec[:, :].rearrange("p (r q a) -> p r q a", r=2, a=1).to_broadcast([P, 2, 8, HD]),
                                                ALU.mult).then_inc(o_divided, 1)
                    if k == 3:
                        dve.wait_ge(o_divided, u + 1)
                        if u:
                            dve.wait_ge(ctx_lo, u)
                        nc.vector.transpose(o_t[:, :], o_div[:, :]).then_inc(o_back, 1)
                if x[0] == "wo":
                    _, n, t = x
                    tile = TT * (n % B) + t
                    dve.wait_ge(wk_filled, wk[x] + 1)
                    nc.vector.tensor_tensor(x_res[:, tile, :], x_res[:, tile, :], banks[:, work_bank(x), :],
                                            ALU.add).then_inc(wk_emptied, 1)
                if x[0] == "hidden":
                    _, L, c = x
                    k = ups[("up", L, c)]
                    cc = c % CHUNKS[L]
                    if L == 1:
                        dve.wait_ge(gate_done, k - 2 * CHUNKS[0] + 1)
                        nc.vector.scalar_tensor_tensor(out=hid_f[:, c % 2, :], in0=banks[:, HID[2 * (c % 2) + 1], :],
                                                       scalar=bias_up[:, 20 + cc:21 + cc], in1=gate_f[:, c % 2, :],
                                                       op0=ALU.add, op1=ALU.mult).then_inc(full_done, 1)
                if x[0] == "hidden_lo":
                    _, L, c = x
                    k = ups[("up", L, c)]
                    hid_hi, hid_lo = hid_part[L]
                    dve.wait_ge(hi_done, k + 1)
                    dve.wait_ge(full_done, k + 1)
                    if k >= 2:
                        dve.wait_ge(down_done, k - 1)
                    nc.vector.tensor_tensor(hid_lo[:, c % 2, :], hid_f[:, c % 2, :], hid_hi[:, c % 2, :].bitcast(F32),
                                            ALU.subtract).then_inc(lo_done, 1)
                if x[0] == "add":
                    _, L, h = x
                    for t in range(HT):
                        if t < HT - 1:
                            dve.wait_ge(acc_filled, (HT - 1) * adds[x] + t + 1)
                        else:
                            dve.wait_ge(down_done, downs[("down", L, (h + 1) * CHUNKS[L] - 1)] + 1)
                        nc.vector.tensor_tensor(x_res[:, HT * h + t, :], x_res[:, HT * h + t, :], banks[:, ACC[t], :],
                                                ALU.add).then_inc(added, 1)


_PERM_HEAD = [[4 * (4 * (s // 2) + g) + 2 * (s % 2) + r for g in range(4) for r in range(2)] for s in range(S)]


def _layouts(i):
    def q_rows(head_row):
        return np.array([head_row(_PERM_HEAD[s][h]) + d for s in range(S) for d in range(HD) for h in range(UH)])

    def kd(base):
        return np.array([base(g) + d for d in range(HD) for g in range(NKV)])

    def gd(base):
        return np.array([base(g) + d for g in range(NKV) for d in range(HD)])

    def by_part(w):
        return w.T.reshape(KT, P, -1).transpose(1, 0, 2)

    block = (REP + 2) * HD
    w0 = np.concatenate([i["L0_attn_Wq"][q_rows(lambda h: h * HD)], i["L0_attn_Wk"][kd(lambda g: g * HD)],
                         i["L0_attn_Wv"][gd(lambda g: g * HD)]])
    rows1 = np.concatenate([q_rows(lambda h: (h // REP) * block + (h % REP) * HD),
                            kd(lambda g: g * block + REP * HD), gd(lambda g: g * block + (REP + 1) * HD)])
    w1 = i["L1_attn_w_qkv"][rows1]
    cols = np.array([_PERM_HEAD[s][h] * HD + d for s in range(S) for h in range(UH) for d in range(HD)])
    outs = [by_part(w[:, cols]) for w in (i["L0_attn_Wo"], i["L1_attn_w_dense"])]
    attn = [np.concatenate([by_part(w).reshape(P, KT, 3, 2 * P).transpose(0, 2, 1, 3).reshape(P, -1),
                            o.reshape(P, -1)], 1) for w, o in zip((w0, w1), outs)]
    up0 = i["L0_ffn_W1"].reshape(KT, P, CHUNKS[0], P).transpose(2, 1, 0, 3).reshape(CHUNKS[0], P, -1)
    up1 = i["L1_ffn_w12"].reshape(2, CHUNKS[1], P, KT, P).transpose(1, 4, 0, 3, 2).reshape(CHUNKS[1], P, -1)
    down0 = i["L0_ffn_W2"].reshape(CHUNKS[0], P, D)
    down1 = i["L1_ffn_w3"].T.reshape(CHUNKS[1], P, D)
    up_b = np.concatenate([i["L0_ffn_fc1_bias"].reshape(-1, P), i["L1_ffn_b12"].reshape(-1, P)]).T
    zero = np.zeros(D, np.float32)
    out_b = np.stack([np.stack([i["L0_ffn_fc2_bias"], i["L1_ffn_b3"]]), np.stack([zero, i["L1_attn_b_dense"]])])
    inv = (np.float32(1.0) / np.power(np.float32(1e6), np.arange(0, HD, 2, dtype=np.float32) / np.float32(HD))).astype(np.float32)
    ang = np.outer(inv, np.arange(T, dtype=np.float32)).astype(np.float32)
    cos, sin = np.cos(ang), np.sin(ang)
    row = np.arange(P) // 8
    rope = np.stack([cos[row % 8], np.where((row < 8)[:, None], sin[row % 8], -sin[row % 8])], 1).astype(np.float32)
    c = np.ascontiguousarray
    return {"x": c(i["L0_attn_x"]), "attn0": c(attn[0]), "attn1": c(attn[1]), "up0": c(up0), "up1": c(up1),
            "down0": c(down0), "down1": c(down1), "up_b": c(up_b), "qkv_b": c(i["L1_attn_b_qkv"][rows1].reshape(-1, P).T),
            "out_b": c(out_b), "rope": c(rope)}


def kernel(**inputs):
    import concourse.bacc as _bacc
    from concourse.bass_utils import run_bass_kernel_spmd as _run

    nc = _bacc.Bacc("TRN2", target_bir_lowering=False, num_devices=1)
    arrays = _layouts({k: np.asarray(v) for k, v in inputs.items()})
    a = {k: nc.dram_tensor(f"in_{k}", v.shape, F32, kind="ExternalInput").ap() for k, v in arrays.items()}
    out = nc.dram_tensor("out", (B, T, D), F32, kind="ExternalOutput").ap()
    build(nc, a["x"], [a["attn0"], a["attn1"]], [a["up0"], a["up1"]], [a["down0"], a["down1"]],
          a["up_b"], a["qkv_b"], a["out_b"], a["rope"], out)
    r = _run(nc, [{f"in_{k}": v for k, v in arrays.items()}], core_ids=[0])
    return r.results[0]["out"]
```
